# Optimizing a Trainium2 kernel written in Bass

```python
import numpy as np
import jax
import jax.numpy as jnp

def _softmax(x, axis=-1):
    return jax.nn.softmax(x, axis=axis)

def _gelu(x):
    return jax.nn.gelu(x, approximate=True)

def _silu(x):
    return jax.nn.silu(x)

def _sigmoid(x):
    return jax.nn.sigmoid(x)

def _layernorm(x, axis=-1, eps=1e-05):
    m = jnp.mean(x, axis=axis, keepdims=True)
    v = jnp.var(x, axis=axis, keepdims=True)
    return (x - m) / jnp.sqrt(v + eps)

def _scatter_add(tgt, idx, src, axis=0):
    return tgt.at[idx].add(src)

def _segment_sum(src, seg, n):
    return jax.ops.segment_sum(src, seg, n)
kernel_name = 'mk_adaln_ffn_d2_seqx_r8_45d0e5'

def setup_inputs(seed: int=0):
    np.random.seed(seed)
    _w = jnp.asarray

    def _rec_inputs():
        import jax
        import jax.numpy as jnp
        _rk = jax.random.key(seed)
        x = 7.22e-05 + 1 * jax.random.normal(jax.random.fold_in(_rk, 1), (8, 128, 512), jnp.float32)
        _lenS = 128 - jax.random.randint(jax.random.fold_in(_rk, 7), (8,), 0, max(1, 128 // 4) + 1, jnp.int32)
        _lenS2 = 128 - jax.random.randint(jax.random.fold_in(_rk, 8), (8,), 0, max(1, 128 // 4) + 1, jnp.int32)
        itok_B_2_6 = jax.random.randint(jax.random.fold_in(_rk, 11), (8,), 2, 7, jnp.int32)
        itok_B_0_7 = jax.random.randint(jax.random.fold_in(_rk, 12), (8,), 0, 8, jnp.int32)
        return (x, itok_B_2_6, itok_B_0_7)
    x, itok_B_2_6, itok_B_0_7 = _rec_inputs()

    def _L0_cond_setup():
        import jax, jax.numpy as jnp
        import numpy as np
        B, N, H, F = (4, 64, 512, 1376)
        L, R, RANK = (1, 16, 16)
        SCALE = 0.5
        key = jax.random.key(seed)
        ks = jax.random.split(key, 12)
        nrm = lambda k, shape, fan: jax.random.normal(k, shape, jnp.float32) * fan ** (-0.5)
        inp = {'x': jax.random.normal(ks[0], (B, N, H), jnp.float32), 'W_gate': nrm(ks[1], (F, H), H), 'W_up': nrm(ks[2], (F, H), H), 'W_down': nrm(ks[3], (H, F), F), 'A_gate': nrm(ks[4], (L, R, RANK, H), H), 'B_gate': nrm(ks[5], (L, R, F, RANK), RANK), 'A_up': nrm(ks[6], (L, R, RANK, H), H), 'B_up': nrm(ks[7], (L, R, F, RANK), RANK), 'A_down': nrm(ks[8], (L, R, RANK, F), F), 'B_down': nrm(ks[9], (L, R, H, RANK), RANK), 'lora_indices': jax.random.randint(ks[10], (B,), 0, R), 'layer_idx': 0}
        return inp
    _L0_cond_all = _L0_cond_setup()
    _L0_cond_in = {k: v for k, v in _L0_cond_all.items() if k in ('W_gate', 'W_up', 'W_down', 'A_gate', 'B_gate', 'A_up', 'B_up', 'A_down', 'B_down')}
    del _L0_cond_all

    def _L0_ffn_setup():
        import jax, jax.numpy as jnp
        import numpy as np
        BLOCK_SIZE = 64
        OUT_F, IN_F = (512, 512)

        def dequantize(qweights, scales, block_size=BLOCK_SIZE):
            shape = qweights.shape
            n = qweights.size
            flat = qweights.reshape(-1)
            pad = -n % block_size
            if pad:
                flat = jnp.pad(flat, (0, pad))
            blocks = flat.reshape(-1, block_size).astype(scales.dtype) * scales
            return blocks.reshape(-1)[:n].reshape(shape)
        key = jax.random.key(seed)
        k_x, k_w, k_s, k_b = jax.random.split(key, 4)
        x = jax.random.normal(k_x, (4, 256, 512), dtype=jnp.float32)
        quantized_weights = jax.random.randint(k_w, (OUT_F, IN_F), -128, 128, dtype=jnp.int32).astype(jnp.int8)
        n_blocks = (OUT_F * IN_F + BLOCK_SIZE - 1) // BLOCK_SIZE
        scale_values = jax.random.uniform(k_s, (n_blocks, 1), minval=0.001, maxval=0.02, dtype=jnp.float32)
        bias = jax.random.normal(k_b, (OUT_F,), dtype=jnp.float32) * 0.02
        return {'x': x, 'quantized_weights': quantized_weights, 'scale_values': scale_values, 'bias': bias}
    _L0_ffn_all = _L0_ffn_setup()
    _L0_ffn_in = {k: v for k, v in _L0_ffn_all.items() if k in ('quantized_weights', 'scale_values', 'bias')}
    del _L0_ffn_all

    def _L1_cond_setup():
        import jax, jax.numpy as jnp
        import numpy as np
        TOP_K = 2
        LANG_BIAS = 5.0
        SCALING = 32.0 / 16.0
        LANGUAGE_PAD_ID = -1
        key = jax.random.key(seed)
        ks = jax.random.split(key, 6)
        B, T, D, O, E, R = (4, 256, 512, 512, 8, 16)
        x = jax.random.normal(ks[0], (B, T, D), dtype=jnp.float32)
        language_ids = jax.random.randint(ks[1], (B,), 0, E).astype(jnp.int64)
        W = jax.random.normal(ks[2], (O, D), dtype=jnp.float32) * (1.0 / np.sqrt(D))
        Wr = jax.random.normal(ks[3], (E, D), dtype=jnp.float32) * (1.0 / np.sqrt(D))
        A = jax.random.normal(ks[4], (E, R, D), dtype=jnp.float32) * (1.0 / np.sqrt(D))
        Bm = jax.random.normal(ks[5], (O, R), dtype=jnp.float32) * 0.0
        Bm = jnp.broadcast_to(Bm, (E, O, R)) + jax.random.normal(ks[5], (E, O, R), dtype=jnp.float32) * 0.02
        return {'x': x, 'language_ids': language_ids, 'W': W, 'Wr': Wr, 'A': A, 'B': Bm}
    _L1_cond_all = _L1_cond_setup()
    _L1_cond_in = {k: v for k, v in _L1_cond_all.items() if k in ('W', 'Wr', 'A', 'B')}
    del _L1_cond_all

    def _L1_ffn_setup():
        import jax, jax.numpy as jnp
        import numpy as np
        NUM_EXPERTS = 8
        TOP_K = 2
        RANK = 16
        LORA_ALPHA = 32
        SCALING = LORA_ALPHA / RANK
        key = jax.random.key(seed)
        ks = jax.random.split(key, 6)
        B, S, D_IN, D_OUT = (4, 256, 512, 512)
        x = jax.random.normal(ks[0], (B, S, D_IN), dtype=jnp.float32)
        W_base = jax.random.normal(ks[1], (D_OUT, D_IN), dtype=jnp.float32) * 0.02
        b_base = jax.random.normal(ks[2], (D_OUT,), dtype=jnp.float32) * 0.02
        W_router = jax.random.normal(ks[3], (NUM_EXPERTS, D_IN), dtype=jnp.float32) * 0.02
        A = jax.random.normal(ks[4], (NUM_EXPERTS, RANK, D_IN), dtype=jnp.float32) * 0.02
        Bm = jax.random.normal(ks[5], (D_OUT, RANK), dtype=jnp.float32) * 0.02
        Bm = jnp.broadcast_to(Bm, (NUM_EXPERTS, D_OUT, RANK)) * jnp.arange(1, NUM_EXPERTS + 1, dtype=jnp.float32)[:, None, None] * 0.2
        return {'x': x, 'W_base': W_base, 'b_base': b_base, 'W_router': W_router, 'A': A, 'B': Bm}
    _L1_ffn_all = _L1_ffn_setup()
    _L1_ffn_in = {k: v for k, v in _L1_ffn_all.items() if k in ('W_base', 'b_base', 'W_router', 'A', 'B')}
    del _L1_ffn_all
    return {'x': x, 'itok_B_2_6': itok_B_2_6, 'itok_B_0_7': itok_B_0_7, 'L0_cond_W_gate': _L0_cond_in['W_gate'], 'L0_cond_W_up': _L0_cond_in['W_up'], 'L0_cond_W_down': _L0_cond_in['W_down'], 'L0_cond_A_gate': _L0_cond_in['A_gate'], 'L0_cond_B_gate': _L0_cond_in['B_gate'], 'L0_cond_A_up': _L0_cond_in['A_up'], 'L0_cond_B_up': _L0_cond_in['B_up'], 'L0_cond_A_down': _L0_cond_in['A_down'], 'L0_cond_B_down': _L0_cond_in['B_down'], 'L0_ffn_quantized_weights': _L0_ffn_in['quantized_weights'], 'L0_ffn_scale_values': _L0_ffn_in['scale_values'], 'L0_ffn_bias': _L0_ffn_in['bias'], 'L1_cond_W': _L1_cond_in['W'], 'L1_cond_Wr': _L1_cond_in['Wr'], 'L1_cond_A': _L1_cond_in['A'], 'L1_cond_B': _L1_cond_in['B'], 'L1_ffn_W_base': _L1_ffn_in['W_base'], 'L1_ffn_b_base': _L1_ffn_in['b_base'], 'L1_ffn_W_router': _L1_ffn_in['W_router'], 'L1_ffn_A': _L1_ffn_in['A'], 'L1_ffn_B': _L1_ffn_in['B']}

def reference(x, itok_B_2_6, itok_B_0_7, L0_cond_W_gate, L0_cond_W_up, L0_cond_W_down, L0_cond_A_gate, L0_cond_B_gate, L0_cond_A_up, L0_cond_B_up, L0_cond_A_down, L0_cond_B_down, L0_ffn_quantized_weights, L0_ffn_scale_values, L0_ffn_bias, L1_cond_W, L1_cond_Wr, L1_cond_A, L1_cond_B, L1_ffn_W_base, L1_ffn_b_base, L1_ffn_W_router, L1_ffn_A, L1_ffn_B):
    import jax
    import jax.numpy as jnp

    def _L0_cond_ref(x, W_gate, W_up, W_down, A_gate, B_gate, A_up, B_up, A_down, B_down, lora_indices, layer_idx):
        import jax, jax.numpy as jnp
        import numpy as np
        B, N, H, F = (4, 64, 512, 1376)
        L, R, RANK = (1, 16, 16)
        SCALE = 0.5

        def lora_add(base, inp, A, B):
            Ab = A[layer_idx][lora_indices]
            Bb = B[layer_idx][lora_indices]
            t = jnp.einsum('bri,bni->bnr', Ab, inp)
            return base + jnp.einsum('bor,bnr->bno', Bb, t) * SCALE
        gate = lora_add(jnp.einsum('bnh,fh->bnf', x, W_gate), x, A_gate, B_gate)
        up = lora_add(jnp.einsum('bnh,fh->bnf', x, W_up), x, A_up, B_up)
        act = jax.nn.silu(gate) * up
        down = lora_add(jnp.einsum('bnf,hf->bnh', act, W_down), act, A_down, B_down)
        return down

    def _L0_ffn_ref(x, quantized_weights, scale_values, bias):
        import jax, jax.numpy as jnp
        import numpy as np
        BLOCK_SIZE = 64
        OUT_F, IN_F = (512, 512)

        def dequantize(qweights, scales, block_size=BLOCK_SIZE):
            shape = qweights.shape
            n = qweights.size
            flat = qweights.reshape(-1)
            pad = -n % block_size
            if pad:
                flat = jnp.pad(flat, (0, pad))
            blocks = flat.reshape(-1, block_size).astype(scales.dtype) * scales
            return blocks.reshape(-1)[:n].reshape(shape)
        w_fp = dequantize(quantized_weights, scale_values)
        return jnp.einsum('bsi,oi->bso', x, w_fp) + bias

    def _L1_cond_ref(x, language_ids, W, Wr, A, B):
        import jax, jax.numpy as jnp
        import numpy as np
        TOP_K = 2
        LANG_BIAS = 5.0
        SCALING = 32.0 / 16.0
        LANGUAGE_PAD_ID = -1
        base = jnp.einsum('btd,od->bto', x, W)
        E = Wr.shape[0]
        logits = jnp.einsum('btd,ed->bte', x.astype(jnp.float32), Wr.astype(jnp.float32))
        expert_targets = language_ids
        valid = expert_targets >= 0
        tgt = jnp.where(valid, expert_targets, 0)
        bias = jax.nn.one_hot(tgt, E, dtype=logits.dtype) * LANG_BIAS
        bias = jnp.where(valid[:, None], bias, 0.0)
        logits = logits + bias[:, None, :]
        topw, topi = jax.lax.top_k(logits, TOP_K)
        weights = jax.nn.softmax(topw, axis=-1)
        gates = jnp.sum(jax.nn.one_hot(topi, E, dtype=weights.dtype) * weights[..., None], axis=-2)
        gates = gates.astype(x.dtype)
        h = jnp.einsum('btd,erd->bter', x, A)
        lora_out = jnp.einsum('bter,bte,eor->bto', h, gates, B)
        return base + SCALING * lora_out

    def _L1_ffn_ref(x, W_base, b_base, W_router, A, B):
        import jax, jax.numpy as jnp
        import numpy as np
        NUM_EXPERTS = 8
        TOP_K = 2
        RANK = 16
        LORA_ALPHA = 32
        SCALING = LORA_ALPHA / RANK
        bs, seq, d_in = x.shape
        T = bs * seq
        xf = x.reshape(T, d_in)
        base = xf @ W_base.T + b_base
        logits = xf @ W_router.T
        rw, sel = jax.lax.top_k(logits, TOP_K)
        rw = jax.nn.softmax(rw, axis=-1)
        onehot = jax.nn.one_hot(sel, NUM_EXPERTS, dtype=rw.dtype)
        w = jnp.einsum('tk,tke->te', rw, onehot)
        h = jnp.einsum('td,erd->ter', xf, A)
        lora = jnp.einsum('ter,te,eor->to', h, w, B) * SCALING
        return (base + lora).reshape(bs, seq, -1)
    x = x + _L0_ffn_ref(_L0_cond_ref(x, L0_cond_W_gate, L0_cond_W_up, L0_cond_W_down, L0_cond_A_gate, L0_cond_B_gate, L0_cond_A_up, L0_cond_B_up, L0_cond_A_down, L0_cond_B_down, itok_B_2_6, 0), L0_ffn_quantized_weights, L0_ffn_scale_values, L0_ffn_bias)
    x = x + _L1_ffn_ref(_L1_cond_ref(x, itok_B_0_7, L1_cond_W, L1_cond_Wr, L1_cond_A, L1_cond_B), L1_ffn_W_base, L1_ffn_b_base, L1_ffn_W_router, L1_ffn_A, L1_ffn_B)
    return x

_drawn_inputs = setup_inputs


def setup_inputs(seed=0):
    import zlib

    import numpy as np

    out = dict(_drawn_inputs(seed))
    spreads = {}
    factors = {'L0_ffn_bias': 43.351, 'L1_ffn_b_base': 64.0}
    for name, (base, spread) in spreads.items():
        noise = np.random.default_rng([zlib.crc32(name.encode()), seed]).standard_normal(out[name].shape)
        drawn = base * np.exp(spread * noise) if base else spread * noise
        out[name] = jnp.asarray(drawn.astype(out[name].dtype))
    for name, factor in factors.items():
        out[name] = (out[name] * factor).astype(out[name].dtype)
    return out
```

```python
from contextlib import ExitStack

import concourse.bass as bass
from concourse import mybir

F32 = mybir.dt.float32
F32R = mybir.dt.float32r
I32 = mybir.dt.int32
I8 = mybir.dt.int8
U32 = mybir.dt.uint32
ALU = mybir.AluOpType
ACT = mybir.ActivationFunctionType

P = 128
B = 8
D = 512
KD = D // P
HALVES = 2
HS = B // HALVES
TOK = HS * P
F = 1376
FC = -(-F // P)
RANK = 16
ADAPTERS = 16
E = 8
PAIR = 2 * RANK
GU = 2 * KD * P
LW = KD * D + KD * P + D
LORA_SCALE = 0.5
LANG_BIAS = 5.0
STEPS = HALVES * FC
LOOPED = 4
C_PAIR, C_DOWN, C_ID, C_IOTA, C_BIAS = 0, 256, 768, 896, 904
CONSTS = 912


def build(nc, x, ids, consts, a_gu, b_gu, a_dn, b_dn, w_ffn, q_w, q_scale, routers, l1_w, out):
    with ExitStack() as ctx:
        def sem(name):
            return ctx.enter_context(nc.semaphore(name))

        def sb(name, shape, dt=F32, where=ctx):
            return where.enter_context(nc.sbuf_tensor(name, shape, dt))

        ids_sb = sb("ids_sb", [1, 8], I32)
        lang_i = sb("lang_i", [P, B], I32)
        lang_f = sb("lang_f", [P, B])
        cst = sb("cst", [P, CONSTS])
        XF = sb("XF", [P, KD, HALVES * TOK])
        PH = sb("PH", [P, KD, HALVES * TOK], F32R)
        PL = sb("PL", [P, KD, HALVES * TOK], F32R)
        l1_raw = sb("l1_raw", [P, LW])
        q_i32 = sb("q_i32", [P, KD, D // 4], I32)
        q_sc = sb("q_sc", [P, KD, D])
        q_f = sb("q_f", [P, D])
        QH = sb("QH", [P, KD, D], F32R)
        QL = sb("QL", [P, KD, D], F32R)
        rt_raw = sb("rt_raw", [P, 2, KD, E])
        RT = sb("RT", [P, 2, KD, 2, E], F32R)
        lang_bias = sb("lang_bias", [P, B, E])
        pair_mask = cst[:, C_PAIR:C_PAIR + 256]
        down_mask = cst[:, C_DOWN:C_DOWN + TOK]
        ident = cst[:, C_ID:C_ID + P]
        iota_e = cst[:, C_IOTA:C_IOTA + E]

        early = ctx.enter_context(ExitStack())
        w_raw = [sb(f"w_raw{i}", [P, GU + D], where=early) for i in range(2)]
        GUH = [sb(f"GUH{i}", [P, 2, KD, P], F32R, early) for i in range(2)]
        GUL = [sb(f"GUL{i}", [P, 2, KD, P], F32R, early) for i in range(2)]
        WDH = [sb(f"WDH{i}", [P, D], F32R, early) for i in range(2)]
        WDL = [sb(f"WDL{i}", [P, D], F32R, early) for i in range(2)]
        b_raw = [sb(f"b_raw{i}", [PAIR, 2, 2 * P], where=early) for i in range(2)]
        BGU = [sb(f"BGU{i}", [3 * PAIR, 2, 2 * P], F32R, early) for i in range(2)]
        ad_raw = sb("ad_raw", [P, B, FC, RANK], where=early)
        ADN = [sb(f"ADN{i}", [P, 2, HS * RANK], F32R, early) for i in range(2)]
        bd_raw = sb("bd_raw", [HS * RANK, HALVES, D], where=early)
        BD1 = sb("BD1", [P, HALVES, D], F32R, early)
        BD2 = sb("BD2", [P, HALVES, D], F32R, early)
        a_raw = sb("a_raw", [P, B, 2 * KD, RANK], where=early)
        AH = sb("AH", [P, HALVES, 2 * KD, HS, RANK], F32R, early)
        AL = sb("AL", [P, HALVES, 2 * KD, HS, RANK], F32R, early)
        TM = sb("TM", [P, TOK], where=early)
        TH = sb("TH", [P, TOK], F32R, early)
        TL = sb("TL", [P, TOK], F32R, early)
        RGU = sb("RGU", [3 * PAIR, HALVES, 2, 2, 2 * P], F32R, early)
        TDM = sb("TDM", [P, TOK], where=early)
        TD1 = sb("TD1", [P, TOK], F32R, early)
        TD2 = sb("TD2", [P, TOK], F32R, early)
        sil = [sb(f"sil{i}", [P, TOK], where=early) for i in range(2)]
        act_f = [sb(f"act_f{i}", [P, TOK], where=early) for i in range(2)]
        ACH = [sb(f"ACH{i}", [P, TOK], F32R, early) for i in range(2)]
        ACL = [sb(f"ACL{i}", [P, TOK], F32R, early) for i in range(2)]
        early.close()

        UH = sb("UH", [P, KD, HALVES * TOK], F32R)
        UL = sb("UL", [P, KD, HALVES * TOK], F32R)
        LH = [sb(f"LH{i}", [P, LW], F32R) for i in range(2)]
        LL = [sb(f"LL{i}", [P, LW], F32R) for i in range(2)]
        hid = sb("hid", [P, TOK])
        gh = sb("gh", [P, TOK])
        GHH = sb("GHH", [P, TOK], F32R)
        GHL = sb("GHL", [P, TOK], F32R)
        part_l = sb("part_l", [P, HS, E])
        logit = sb("logit", [P, HS, E])
        top8 = sb("top8", [P, HS, E])
        top8_i = sb("top8_i", [P, HS, E], U32)
        top2_f = sb("top2_f", [P, HS, 2])
        gap = sb("gap", [P, HS, 1])
        gap_e = sb("gap_e", [P, HS, 1])
        half_sum = sb("half_sum", [P, HS, 1])
        gate2 = sb("gate2", [P, HS, 2])
        onehot = sb("onehot", [P, HS, 2, E])
        chosen = sb("chosen", [P, HS, 2, E])
        gates = sb("gates", [P, HS, E])
        gates_r = sb("gates_r", [P, HS, E, RANK])

        PB = [ctx.enter_context(nc.psum_tensor(f"bank{i}", [P, TOK], F32)) for i in range(8)]
        GATE, UP, TDN, TGU = PB[4], PB[5], PB[6], PB[7]
        ROUTE, HID, GATET = PB[4], PB[5], PB[6]

        ids_in, x_in, cst_in, lang_in = sem("ids_in"), [sem(f"x_in{k}") for k in range(KD + 1)], sem("cst_in"), sem("lang_in")
        a_in, ad_in, bd_in, q_in, rt_in = sem("a_in"), sem("ad_in"), sem("bd_in"), sem("q_in"), sem("rt_in")
        w_in, b_in = [sem("w_in0"), sem("w_in1")], [sem("b_in0"), sem("b_in1")]
        l1_in = [sem("l1_in0"), sem("l1_in1")]
        x_hi, x_split = sem("x_hi"), sem("x_split")
        a_hi, a_split = sem("a_hi"), sem("a_split")
        gu_hi, gu_split, b_hi, b_split = sem("gu_hi"), sem("gu_split"), sem("b_hi"), sem("b_split")
        dn_hi, dn_split = sem("dn_hi"), sem("dn_split")
        bd_hi, bd_split = sem("bd_hi"), sem("bd_split")
        t_done, t_masked, t_hi, t_rest, r_hi, r_rest = (sem(n) for n in ("t_done", "t_masked", "t_hi", "t_rest", "r_hi", "r_rest"))
        gu_done, silu_done, act_done, act_hi, act_split = (sem(n) for n in ("gu_done", "silu_done", "act_done", "act_hi", "act_split"))
        dn_done, td_done, td_masked, td_hi, td_split, td_shift = (sem(n) for n in ("dn_done", "td_done", "td_masked", "td_hi", "td_split", "td_shift"))
        d_done, d_hi, d_split = sem("d_done"), sem("d_hi"), sem("d_split")
        q_prod, q_hi, q_split, rt_hi, rt_split = (sem(n) for n in ("q_prod", "q_hi", "q_split", "rt_hi", "rt_split"))
        f_done, x2_done, u_hi, u_split = (sem(n) for n in ("f_done", "x2_done", "u_hi", "u_split"))
        l1_hi, l1_split = sem("l1_hi"), sem("l1_split")
        route_done, gap_done, exp_done, gates_done = (sem(n) for n in ("route_done", "gap_done", "exp_done", "gates_done"))
        hid_done, hid_copied, gatet_done, gh_done, gh_hi, gh_split = (sem(n) for n in ("hid_done", "hid_copied", "gatet_done", "gh_done", "gh_hi", "gh_split"))
        o_done, y_hi, y_split, x3_done, stored = (sem(n) for n in ("o_done", "y_hi", "y_split", "x3_done", "stored"))
        chain = sem("chain")

        def half(h):
            return slice(h * TOK, (h + 1) * TOK)

        def f32(ap):
            return ap.bitcast(F32)

        def dyn(i):
            return bass.DynSlice(i, 1)

        def steps(eng, h, step, first=2, turns=LOOPED):
            with eng.Fori(0, turns) as i:
                for j in range(2):
                    k = h * FC + first + j
                    step(i * 2 + (first + j), i * 2 + k, k % 2, i + k // 2)

        def one_step(h, c, step):
            s = h * FC + c
            step(c, s, s % 2, s // 2)

        block = ctx.enter_context(nc.Block())

        @block.sync
        def _(sp):
            sp.dma_start(ids_sb[:, :], ids[0:1, :]).then_inc(ids_in, 16)
            for k in range(KD):
                sp.dma_start(XF[:, k, half(0)], x[0, :, k, :]).then_inc(x_in[k], 16)
            sp.wait_ge(ids_in, 16)
            who = [sp.value_load(ids_sb[0:1, b:b + 1], min_val=0, max_val=ADAPTERS - 1) for b in range(B)]
            for b in range(B):
                sp.dma_start(a_raw[:, b:b + 1, :, :], a_gu[dyn(who[b])].rearrange("a p k r -> p a k r")).then_inc(a_in, 16)

            def load_b(c, par, h):
                for i in range(HS):
                    sp.dma_start(b_raw[par][RANK * (i % 2):RANK * (i % 2) + RANK, i // 2, :],
                                 b_gu[dyn(who[h * HS + i]), c].rearrange("a c r n -> r (a c n)")).then_inc(b_in[par], 16)

            load_b(slice(0, 1), 0, 0)
            sp.dma_start(w_raw[1][:, :], w_ffn[1]).then_inc(w_in[1], 16)
            load_b(slice(1, 2), 1, 0)
            sp.dma_start(XF[:, :, half(1)], x[1]).then_inc(x_in[KD], 16)
            for b in range(B):
                sp.dma_start(ad_raw[:, b:b + 1, :, :], a_dn[dyn(who[b])].rearrange("a p c r -> p a c r")).then_inc(ad_in, 16)
            for b in range(B):
                sp.dma_start(bd_raw[RANK * (b % HS):RANK * (b % HS) + RANK, b // HS, :],
                             b_dn[dyn(who[b])].rearrange("a r n -> r (a n)")).then_inc(bd_in, 16)

            def load(h):
                def step(c, s, par, turn):
                    sp.wait_ge(dn_split, s - 1)
                    sp.wait_ge(gu_split, s - 1)
                    sp.dma_start(w_raw[par][:, :], w_ffn[dyn(c)].rearrange("a p n -> p (a n)")).then_inc(w_in[par], 16)
                    sp.wait_ge(b_split, s - 1)
                    load_b(dyn(c), par, h)
                return step

            steps(sp, 0, load(0))
            one_step(0, FC - 1, load(0))
            sp.dma_start(q_i32[:, :, :], q_w[:, :, :]).then_inc(q_in, 16)
            sp.dma_start(q_sc[:, :, :], q_scale[:, :, :]).then_inc(q_in, 16)
            sp.dma_start(rt_raw[:, :, :, :], routers[:, :, :, :]).then_inc(rt_in, 16)
            sp.dma_start(l1_raw[:, :], l1_w[0]).then_inc(l1_in[0], 16)
            steps(sp, 1, load(1), first=0, turns=LOOPED + 1)
            one_step(1, FC - 1, load(1))
            sp.wait_ge(l1_split, 4)
            sp.dma_start(l1_raw[:, :], l1_w[1]).then_inc(l1_in[1], 16)
            for h in range(HALVES):
                for o in range(KD):
                    sp.wait_ge(x3_done, h * KD + o + 1)
                    sp.dma_start(out[h, :, o, :], XF[:, o, half(h)]).then_inc(stored, 16)
            sp.wait_ge(stored, 16 * HALVES * KD)

        @block.scalar
        def _(act):
            def high(dst, src):
                return nc.scalar.activation(dst, src, ACT.Copy)

            act.dma_start(w_raw[0][:, :], w_ffn[0]).then_inc(w_in[0], 16)
            act.dma_start(cst[:, :], consts[:, :]).then_inc(cst_in, 16)
            act.dma_start(lang_i[:, :], ids[1:2, :].partition_broadcast(P)).then_inc(lang_in, 16)

            def split_x(h):
                for k in range(KD):
                    act.wait_ge(x_in[KD if h else k], 16)
                    high(PH[:, k, half(h)], XF[:, k, half(h)]).then_inc(x_hi, 1)

            def split_b(s, par, turn):
                act.wait_ge(b_in[par], (turn + 1) * 16 * HS)
                high(BGU[par][0:PAIR, :, :], b_raw[par][:, :, :])
                high(BGU[par][PAIR:2 * PAIR, :, :], b_raw[par][:, :, :]).then_inc(b_hi, 1)

            def rhs_gu(h):
                act.wait_ge(t_masked, h + 1)
                if h:
                    act.wait_ge(r_hi, h)
                high(TH[:, :], TM[:, :]).then_inc(t_hi, 1)
                act.wait_ge(t_rest, h + 1)
                for g in range(2):
                    for p in range(2):
                        q = PAIR * (2 * g + p)
                        last = high(RGU[PAIR:2 * PAIR, h, p, g, :], f32(TL[q:q + PAIR, 2 * P * p:2 * P * p + 2 * P]))
                last.then_inc(r_rest, 1)

            def step_for(h):
                def step(c, s, par, turn, more=True):
                    if not isinstance(s, int) or s >= 2:
                        act.wait_ge(dn_done, s - 1)
                    act.wait_ge(w_in[par], (turn + 1) * 16)
                    cs = slice(c, c + 1) if isinstance(c, int) else dyn(c)
                    high(ADN[par][:, 0, :].rearrange("p (b r) -> p b r", r=RANK),
                         ad_raw[:, h * HS:(h + 1) * HS, cs, :].rearrange("p b c r -> p b (c r)"))
                    high(WDH[par][:, :], w_raw[par][:, GU:GU + D]).then_inc(dn_hi, 1)
                    if more:
                        nxt, nturn = 1 - par, turn + par
                        act.wait_ge(w_in[nxt], (nturn + 1) * 16)
                        if not isinstance(s, int) or s >= 1:
                            act.wait_ge(gu_done, s)
                        high(GUH[nxt][:, :, :, :].rearrange("p g k m -> p (g k m)"), w_raw[nxt][:, 0:GU]).then_inc(gu_hi, 1)
                        split_b(s + 1, nxt, nturn)
                    act.wait_ge(gu_done, s + 1)
                    nc.scalar.activation(sil[par][:, :], GATE[:, :], ACT.Silu).then_inc(silu_done, 1)
                    act.wait_ge(act_done, s + 1)
                    high(ACH[par][:, :], act_f[par][:, :]).then_inc(act_hi, 1)
                return step

            def cond_out(h):
                act.wait_ge(td_masked, h + 1)
                high(TD1[:, :], TDM[:, :]).then_inc(td_hi, 1)
                high(TD2[64:128, :], TDM[0:64, :]).then_inc(td_shift, 1)
                for o in range(KD):
                    act.wait_ge(d_done, h * KD + o + 1)
                    high(PH[:, o, half(h)], PB[o][:, :]).then_inc(d_hi, 1)

            def split_q(ks):
                for k in ks:
                    act.wait_ge(q_prod, k + 1)
                    high(QH[:, k, :], q_f[:, :]).then_inc(q_hi, 1)

            split_x(0)
            act.wait_ge(w_in[0], 16)
            high(GUH[0][:, :, :, :].rearrange("p g k m -> p (g k m)"), w_raw[0][:, 0:GU]).then_inc(gu_hi, 1)
            act.wait_ge(a_in, 16 * B)
            for h in range(HALVES):
                high(AH[:, h].rearrange("p k b r -> p b k r"), a_raw[:, h * HS:(h + 1) * HS]).then_inc(a_hi, 1)
            split_b(0, 0, 0)
            rhs_gu(0)
            act.wait_ge(ad_in, 16 * B)
            one_step(0, 0, step_for(0))
            split_x(1)
            act.wait_ge(bd_in, 16 * B)
            high(BD1[0:64, :, :], bd_raw[:, :, :])
            high(BD1[64:128, :, :], bd_raw[:, :, :])
            high(BD2[0:64, :, :], bd_raw[:, :, :]).then_inc(bd_hi, 1)
            one_step(0, 1, step_for(0))
            rhs_gu(1)
            steps(act, 0, step_for(0))
            one_step(0, FC - 1, step_for(0))
            one_step(1, 0, step_for(1))
            cond_out(0)
            one_step(1, 1, step_for(1))
            act.wait_ge(rt_in, 16)
            for i in range(2):
                high(RT[:, i, :, 0, :], rt_raw[:, i, :, :]).then_inc(rt_hi, 1)
            split_q(range(0, 2))
            steps(act, 1, step_for(1))
            split_q(range(2, KD))
            one_step(1, FC - 1, lambda *a: step_for(1)(*a, more=False))
            cond_out(1)

            def split_l1(i, q):
                n = LW // 4
                if q == 0:
                    act.wait_ge(l1_in[i], 16)
                high(LH[i][:, q * n:(q + 1) * n], l1_raw[:, q * n:(q + 1) * n]).then_inc(l1_hi, 1)

            for t in range(HALVES * KD):
                h, o = divmod(t, KD)
                act.wait_ge(x2_done, t + 1)
                high(UH[:, o, half(h)], XF[:, o, half(h)]).then_inc(u_hi, 1)
                if h == 0:
                    split_l1(0, o)
            for i in range(2):
                for h in range(HALVES):
                    n = 2 * i + h
                    act.wait_ge(gap_done, n + 1)
                    nc.scalar.activation(gap_e[:, :, :], gap[:, :, :], ACT.Exp).then_inc(exp_done, 1)
                    act.wait_ge(hid_done, n + 1)
                    if n:
                        act.wait_ge(gh_done, n)
                    nc.scalar.activation(hid[:, :], HID[:, :], ACT.Copy).then_inc(hid_copied, 1)
                    if n == 0:
                        split_l1(1, 0)
                        split_l1(1, 1)
                    act.wait_ge(gh_done, n + 1)
                    high(GHH[:, :], gh[:, :]).then_inc(gh_hi, 1)
                    if n == 0:
                        split_l1(1, 2)
                        split_l1(1, 3)
                    for o in range(KD):
                        if i == 0:
                            act.wait_ge(o_done, n * KD + o + 1)
                            high(PH[:, o, half(h)], PB[o][:, :]).then_inc(y_hi, 1)

        @block.vector
        def _(dve):
            count = [0]

            def link(ins):
                count[0] += 1
                ins.then_inc(chain, 1)
                dve.wait_ge(chain, count[0])

            def rest(dst, src, hi):
                return nc.vector.tensor_tensor(dst, src, f32(hi), ALU.subtract)

            def split_x(h):
                for k in range(KD):
                    dve.wait_ge(x_hi, h * KD + k + 1)
                    rest(PL[:, k, half(h)], XF[:, k, half(h)], PH[:, k, half(h)]).then_inc(x_split, 1)

            def split_b(s, par):
                dve.wait_ge(b_hi, s + 1)
                rest(BGU[par][2 * PAIR:3 * PAIR, :, :], b_raw[par][:, :, :], BGU[par][0:PAIR, :, :]).then_inc(b_split, 1)

            def rhs_gu(h):
                dve.wait_ge(t_done, h + 1)
                if h:
                    dve.wait_ge(t_hi, h)
                nc.vector.tensor_tensor(TM[:, :].rearrange("p (a n) -> p a n", a=2),
                                        TGU[:, :].rearrange("p (a n) -> p a n", a=2),
                                        pair_mask.unsqueeze(1).to_broadcast([P, 2, 256]), ALU.mult).then_inc(t_masked, 1)
                dve.wait_ge(t_hi, h + 1)
                if h:
                    dve.wait_ge(r_rest, h)
                rest(TL[:, :], TM[:, :], TH[:, :]).then_inc(t_rest, 1)
                for g in range(2):
                    for p in range(2):
                        q = PAIR * (2 * g + p)
                        for row in (0, 2 * PAIR):
                            last = nc.vector.tensor_copy(RGU[row:row + PAIR, h, p, g, :],
                                                         TH[q:q + PAIR, 2 * P * p:2 * P * p + 2 * P])
                last.then_inc(r_hi, 1)

            def step_for(h):
                def step(c, s, par, turn, more=True):
                    dve.wait_ge(dn_hi, s + 1)
                    cs = slice(c, c + 1) if isinstance(c, int) else dyn(c)
                    rest(ADN[par][:, 1, :].rearrange("p (b r) -> p b r", r=RANK),
                         ad_raw[:, h * HS:(h + 1) * HS, cs, :].rearrange("p b c r -> p b (c r)"),
                         ADN[par][:, 0, :].rearrange("p (b r) -> p b r", r=RANK))
                    rest(WDL[par][:, :], w_raw[par][:, GU:GU + D], WDH[par][:, :]).then_inc(dn_split, 1)
                    if more:
                        nxt = 1 - par
                        dve.wait_ge(gu_hi, s + 2)
                        rest(GUL[nxt][:, :, :, :].rearrange("p g k m -> p (g k m)"), w_raw[nxt][:, 0:GU],
                             GUH[nxt][:, :, :, :].rearrange("p g k m -> p (g k m)")).then_inc(gu_split, 1)
                        split_b(s + 1, nxt)
                    dve.wait_ge(silu_done, s + 1)
                    nc.vector.tensor_tensor(act_f[par][:, :], sil[par][:, :], UP[:, :], ALU.mult).then_inc(act_done, 1)
                    dve.wait_ge(act_hi, s + 1)
                    rest(ACL[par][:, :], act_f[par][:, :], ACH[par][:, :]).then_inc(act_split, 1)
                return step

            def cond_out(h):
                dve.wait_ge(td_done, h + 1)
                nc.vector.tensor_tensor(TDM[:, :], TDN[:, :], down_mask, ALU.mult).then_inc(td_masked, 1)
                dve.wait_ge(td_hi, h + 1)
                rest(TD2[0:64, :], TDM[0:64, :], TD1[0:64, :]).then_inc(td_split, 1)
                for o in range(KD):
                    dve.wait_ge(d_hi, h * KD + o + 1)
                    rest(PL[:, o, half(h)], PB[o][:, :], PH[:, o, half(h)]).then_inc(d_split, 1)

            def split_q(ks):
                for k in ks:
                    if k:
                        dve.wait_ge(q_split, k)
                    else:
                        dve.wait_ge(q_in, 32)
                    nc.vector.tensor_tensor(q_f[:, :], q_i32[:, k, :].bitcast(I8), q_sc[:, k, :], ALU.mult).then_inc(q_prod, 1)
                    dve.wait_ge(q_hi, k + 1)
                    rest(QL[:, k, :], q_f[:, :], QH[:, k, :]).then_inc(q_split, 1)

            split_x(0)
            dve.wait_ge(gu_hi, 1)
            rest(GUL[0][:, :, :, :].rearrange("p g k m -> p (g k m)"), w_raw[0][:, 0:GU],
                 GUH[0][:, :, :, :].rearrange("p g k m -> p (g k m)")).then_inc(gu_split, 1)
            for h in range(HALVES):
                dve.wait_ge(a_hi, h + 1)
                rest(AL[:, h].rearrange("p k b r -> p b k r"), a_raw[:, h * HS:(h + 1) * HS],
                     AH[:, h].rearrange("p k b r -> p b k r")).then_inc(a_split, 1)
            split_b(0, 0)
            dve.wait_ge(cst_in, 16)
            rhs_gu(0)
            one_step(0, 0, step_for(0))
            split_x(1)
            dve.wait_ge(bd_hi, 1)
            rest(BD2[64:128, :, :], bd_raw[:, :, :], BD1[0:64, :, :]).then_inc(bd_split, 1)
            one_step(0, 1, step_for(0))
            rhs_gu(1)
            steps(dve, 0, step_for(0))
            one_step(0, FC - 1, step_for(0))
            one_step(1, 0, step_for(1))
            cond_out(0)
            one_step(1, 1, step_for(1))
            for i in range(2):
                dve.wait_ge(rt_hi, i + 1)
                rest(RT[:, i, :, 1, :], rt_raw[:, i, :, :], RT[:, i, :, 0, :]).then_inc(rt_split, 1)
            split_q(range(0, 2))
            dve.wait_ge(lang_in, 16)
            link(nc.vector.tensor_copy(lang_f[:, :], lang_i[:, :]))
            link(nc.vector.tensor_tensor(lang_bias[:, :, :], iota_e.unsqueeze(1).to_broadcast([P, B, E]),
                                         lang_f[:, :].unsqueeze(2).to_broadcast([P, B, E]), ALU.is_equal))
            link(nc.vector.tensor_scalar(lang_bias[:, :, :], lang_bias[:, :, :], LANG_BIAS, None, ALU.mult))
            steps(dve, 1, step_for(1))
            split_q(range(2, KD))
            one_step(1, FC - 1, lambda *a: step_for(1)(*a, more=False))
            cond_out(1)

            def split_l1(i, q):
                n = LW // 4
                dve.wait_ge(l1_hi, 4 * i + q + 1)
                rest(LL[i][:, q * n:(q + 1) * n], l1_raw[:, q * n:(q + 1) * n], LH[i][:, q * n:(q + 1) * n]).then_inc(l1_split, 1)

            for t in range(HALVES * KD):
                h, o = divmod(t, KD)
                dve.wait_ge(f_done, t + 1)
                nc.vector.scalar_tensor_tensor(XF[:, o, half(h)], PB[o if h else o + 4][:, :], cst[:, C_BIAS + o:C_BIAS + o + 1],
                                               XF[:, o, half(h)], ALU.add, ALU.add).then_inc(x2_done, 1)
                dve.wait_ge(u_hi, t + 1)
                rest(UL[:, o, half(h)], XF[:, o, half(h)], UH[:, o, half(h)]).then_inc(u_split, 1)
                if h == 0:
                    split_l1(0, o)
            for i in range(2):
                for h in range(HALVES):
                    n = 2 * i + h
                    dve.wait_ge(route_done, n + 1)
                    route = ROUTE[:, 0:HS * 2 * E].rearrange("p (j s e) -> p j s e", s=2, e=E)
                    if i == 0:
                        link(nc.vector.tensor_tensor(part_l[:, :, :], route[:, :, 0, :], lang_bias[:, h * HS:(h + 1) * HS, :], ALU.add))
                    else:
                        link(nc.vector.tensor_copy(part_l[:, :, :], route[:, :, 0, :]))
                    link(nc.vector.tensor_tensor(logit[:, :, :], part_l[:, :, :], route[:, :, 1, :], ALU.add))
                    for j in range(HS):
                        last = nc.vector.max(top8[:, j, :], logit[:, j, :])
                    link(last)
                    nc.vector.tensor_tensor(gap[:, :, :], top8[:, :, 1:2], top8[:, :, 0:1], ALU.subtract).then_inc(gap_done, 1)
                    for j in range(HS):
                        last = nc.vector.max_index(top8_i[:, j, :], top8[:, j, :], logit[:, j, :])
                    link(last)
                    link(nc.vector.tensor_copy(top2_f[:, :, :], top8_i[:, :, 0:2]))
                    nc.vector.tensor_tensor(onehot[:, :, :, :], cst[:, C_IOTA:C_IOTA + E].unsqueeze(1).unsqueeze(1).to_broadcast([P, HS, 2, E]),
                                            top2_f[:, :, :].unsqueeze(3).to_broadcast([P, HS, 2, E]), ALU.is_equal)
                    dve.wait_ge(exp_done, n + 1)
                    link(nc.vector.tensor_scalar(half_sum[:, :, :], gap_e[:, :, :], 0.5, 0.5, ALU.mult, ALU.add))
                    link(nc.vector.reciprocal(gate2[:, :, 0:1], half_sum[:, :, :]))
                    link(nc.vector.tensor_tensor(gate2[:, :, 1:2], gate2[:, :, 0:1], gap_e[:, :, :], ALU.mult))
                    link(nc.vector.tensor_tensor(chosen[:, :, :, :], onehot[:, :, :, :], gate2[:, :, :].unsqueeze(3).to_broadcast([P, HS, 2, E]), ALU.mult))
                    link(nc.vector.tensor_tensor(gates[:, :, :], chosen[:, :, 0, :], chosen[:, :, 1, :], ALU.add))
                    nc.vector.tensor_copy(gates_r[:, :, :, :], gates[:, :, :].unsqueeze(3).to_broadcast([P, HS, E, RANK])).then_inc(gates_done, 1)
                    dve.wait_ge(gatet_done, n + 1)
                    dve.wait_ge(hid_copied, n + 1)
                    nc.vector.tensor_tensor(gh[:, :], hid[:, :], GATET[:, :], ALU.mult).then_inc(gh_done, 1)
                    dve.wait_ge(gh_hi, n + 1)
                    rest(GHL[:, :], gh[:, :], GHH[:, :]).then_inc(gh_split, 1)
                    if n == 0:
                        for q in range(4):
                            split_l1(1, q)
                    for o in range(KD):
                        if i == 0:
                            dve.wait_ge(y_hi, n * KD + o + 1)
                            rest(PL[:, o, half(h)], PB[o][:, :], PH[:, o, half(h)]).then_inc(y_split, 1)
                        else:
                            dve.wait_ge(o_done, n * KD + o + 1)
                            nc.vector.scalar_tensor_tensor(XF[:, o, half(h)], PB[o][:, :], cst[:, C_BIAS + KD + o:C_BIAS + KD + o + 1],
                                                           XF[:, o, half(h)], ALU.add, ALU.add).then_inc(x3_done, 1)

        @block.tensor
        def _(pe):
            def product(bank, wh, wl, mh, ml, start, stop):
                nc.tensor.matmul(bank, wh, mh, start=start, stop=False)
                nc.tensor.matmul(bank, wh, ml, start=False, stop=False)
                return nc.tensor.matmul(bank, wl, mh, start=False, stop=stop)

            def t_gu(h):
                pe.wait_ge(a_split, h + 1)
                pe.wait_ge(x_split, (h + 1) * KD)
                if h:
                    pe.wait_ge(t_masked, h)
                for k in range(KD):
                    cols = [t[:, h].rearrange("p k b r -> p k (b r)")[:, 2 * k:2 * k + 2, :] for t in (AH, AL)]
                    last = product(TGU[:, :], cols[0].rearrange("p g m -> p (g m)"), cols[1].rearrange("p g m -> p (g m)"),
                                   PH[:, k, half(h)], PL[:, k, half(h)], k == 0, k == KD - 1)
                last.then_inc(t_done, 1)

            def gate_up(h, between=None):
                def step(c, s, par, turn):
                    later = not isinstance(s, int) or s >= 1
                    pe.wait_ge(gu_split, s + 1)
                    if isinstance(c, int) and c == 0:
                        pe.wait_ge(x_split, (h + 1) * KD)
                    for g, bank in enumerate((GATE, UP)):
                        if later:
                            pe.wait_ge((silu_done, act_done)[g], s)
                        for k in range(KD):
                            product(bank[:, :], GUH[par][:, g, k, :], GUL[par][:, g, k, :], PH[:, k, half(h)], PL[:, k, half(h)], k == 0, k == KD - 1)
                        if g == 0 and between:
                            between()
                    pe.wait_ge(b_split, s + 1)
                    if isinstance(c, int) and c == 0:
                        pe.wait_ge(r_hi, h + 1)
                        pe.wait_ge(r_rest, h + 1)
                    for g, bank in enumerate((GATE, UP)):
                        for p in range(2):
                            last = nc.tensor.matmul(bank[:, 2 * P * p:2 * P * p + 2 * P], BGU[par][:, p, g * P:(g + 1) * P],
                                                    RGU[:, h, p, g, :], start=False, stop=True, skip_group_check=True)
                    last.then_inc(gu_done, 1)
                return step

            def down(h):
                def step(c, s, par, turn):
                    first = isinstance(c, int) and c == 0
                    final = isinstance(c, int) and c == FC - 1
                    pe.wait_ge(dn_split, s + 1)
                    pe.wait_ge(act_split, s + 1)
                    if first and h:
                        pe.wait_ge(td_masked, h)
                    nc.tensor.matmul(TDN[:, :], ADN[par][:, :, :].rearrange("p a m -> p (a m)"), ACH[par][:, :], start=first, stop=final, skip_group_check=True)
                    last = nc.tensor.matmul(TDN[0:64, :], ADN[par][:, 0, :], ACL[par][:, :], start=False, stop=final, skip_group_check=True)
                    if final:
                        last.then_inc(td_done, 1)
                    for o in range(KD):
                        if first and h:
                            pe.wait_ge(d_split, o + 1)
                        m = slice(o * P, (o + 1) * P)
                        last = product(PB[o][:, :], WDH[par][:, m], WDL[par][:, m], ACH[par][:, :], ACL[par][:, :], first, False)
                    last.then_inc(dn_done, 1)
                return step

            def down_lora(h):
                pe.wait_ge(bd_split, 1)
                pe.wait_ge(td_split, h + 1)
                pe.wait_ge(td_shift, h + 1)
                for o in range(KD):
                    m = slice(o * P, (o + 1) * P)
                    nc.tensor.matmul(PB[o][:, :], BD1[:, h, m], TD1[:, :], start=False, stop=False)
                    nc.tensor.matmul(PB[o][:, :], BD2[:, h, m], TD2[:, :], start=False, stop=True).then_inc(d_done, 1)

            def both(h):
                def step(c, s, par, turn):
                    gate_up(h)(c, s, par, turn)
                    down(h)(c - 1, s - 1, 1 - par, None)
                return step

            one_step(0, 0, gate_up(0, between=lambda: t_gu(0)))
            one_step(0, 1, gate_up(0))
            t_gu(1)
            one_step(0, 0, down(0))
            steps(pe, 0, both(0))
            one_step(0, FC - 1, both(0))
            one_step(1, 0, gate_up(1))
            one_step(0, FC - 1, down(0))
            down_lora(0)
            one_step(1, 1, both(1))
            steps(pe, 1, both(1))
            one_step(1, FC - 1, both(1))
            one_step(1, FC - 1, down(1))
            down_lora(1)

            for h in range(HALVES):
                pe.wait_ge(q_split, KD)
                pe.wait_ge(d_split, (h + 1) * KD)
                for o in range(KD):
                    m = slice(o * P, (o + 1) * P)
                    for k in range(KD):
                        last = product(PB[o if h else o + 4][:, :], QH[:, k, m], QL[:, k, m], PH[:, k, half(h)], PL[:, k, half(h)], k == 0, k == KD - 1)
                    last.then_inc(f_done, 1)

            pe.wait_ge(rt_split, 2)
            pe.wait_ge(cst_in, 16)
            for i in range(2):
                WH, WL = (t[:, 0:KD * D].rearrange("p (k n) -> p k n", k=KD) for t in (LH[i], LL[i]))
                AHI, ALO = (t[:, KD * D:KD * D + KD * P].rearrange("p (k n) -> p k n", k=KD) for t in (LH[i], LL[i]))
                BHI, BLO = (t[:, KD * D + KD * P:LW] for t in (LH[i], LL[i]))
                SH, SL = ((UH, UL), (PH, PL))[i]
                for h in range(HALVES):
                    n = 2 * i + h
                    pe.wait_ge((u_split, y_split)[i], (h + 1) * KD)
                    if n:
                        pe.wait_ge(gates_done, n)
                    for j in range(HS):
                        t = slice(h * TOK + j * P, h * TOK + (j + 1) * P)
                        for k in range(KD):
                            nc.tensor.matmul(ROUTE[:, j * 2 * E:(j + 1) * 2 * E], SH[:, k, t], RT[:, i, k, :, :].rearrange("p s e -> p (s e)"),
                                             start=(k == 0), stop=False, skip_group_check=True)
                            last = nc.tensor.matmul(ROUTE[:, j * 2 * E:j * 2 * E + E], SL[:, k, t], RT[:, i, k, 0, :],
                                                    start=False, stop=(k == KD - 1), skip_group_check=True)
                    last.then_inc(route_done, 1)
                    pe.wait_ge(l1_split, 4 * i + 4)
                    if n:
                        pe.wait_ge(hid_copied, n)
                    for k in range(KD):
                        last = product(HID[:, :], AHI[:, k, :], ALO[:, k, :], SH[:, k, half(h)], SL[:, k, half(h)], k == 0, k == KD - 1)
                    last.then_inc(hid_done, 1)
                    for o in range(KD):
                        m = slice(o * P, (o + 1) * P)
                        if n == 0:
                            pe.wait_ge(x2_done, KD + o + 1)
                        elif n <= 2:
                            pe.wait_ge(y_split, (n - 1) * KD + o + 1)
                        else:
                            pe.wait_ge(x3_done, o + 1)
                        for k in range(KD):
                            product(PB[o][:, :], WH[:, k, m], WL[:, k, m], SH[:, k, half(h)], SL[:, k, half(h)], k == 0, False)
                        if o == 1:
                            pe.wait_ge(gates_done, n + 1)
                            if n:
                                pe.wait_ge(gh_done, n)
                            for j in range(HS):
                                last = nc.tensor.transpose(GATET[:, j * P:(j + 1) * P], gates_r[:, j, :, :].rearrange("p e r -> p (e r)"), ident)
                            last.then_inc(gatet_done, 1)
                    pe.wait_ge(gh_split, n + 1)
                    for o in range(KD):
                        m = slice(o * P, (o + 1) * P)
                        product(PB[o][:, :], BHI[:, m], BLO[:, m], GHH[:, :], GHL[:, :], False, True).then_inc(o_done, 1)


def _const_table(np):
    t = np.zeros((P, CONSTS), np.float32)
    row, col = np.arange(P)[:, None], np.arange(256)[None, :]
    t[:, C_PAIR:C_PAIR + 256] = (row % PAIR // RANK == col // P) * LORA_SCALE
    t[:, C_DOWN:C_DOWN + TOK] = (row % (HS * RANK) // RANK == np.arange(TOK)[None, :] // P) * LORA_SCALE
    t[:, C_ID:C_ID + P] = np.eye(P)
    t[:, C_IOTA:C_IOTA + E] = np.arange(E)
    return t


def kernel(**inputs):
    import numpy as np
    import concourse.bacc as _bacc
    from concourse.bass_utils import run_bass_kernel_spmd as _run

    a = {k: np.asarray(v) for k, v in inputs.items()}

    def tiles(w):
        return w.T.reshape(-1, P, w.shape[0]).transpose(1, 0, 2)

    def padded(w, axis):
        pad = [(0, 0)] * w.ndim
        pad[axis] = (0, FC * P - F)
        return np.pad(w, pad)

    x = a["x"].reshape(HALVES, TOK, KD, P).transpose(0, 3, 2, 1)
    consts = _const_table(np)
    consts[:, C_BIAS:C_BIAS + KD] = a["L0_ffn_bias"].reshape(KD, P).T
    consts[:, C_BIAS + KD:C_BIAS + 2 * KD] = a["L1_ffn_b_base"].reshape(KD, P).T
    gu = [padded(a[f"L0_cond_W_{n}"], 0).reshape(FC, P, KD, P).transpose(0, 3, 2, 1) for n in ("gate", "up")]
    down = padded(a["L0_cond_W_down"], 1).T.reshape(FC, P, D)
    w_ffn = np.concatenate([np.stack(gu, 2).reshape(FC, P, GU), down], 2)
    a_gu = np.stack([a[f"L0_cond_A_{n}"][0].reshape(ADAPTERS, RANK, KD, P) for n in ("gate", "up")], 3)
    a_gu = a_gu.transpose(0, 4, 2, 3, 1).reshape(ADAPTERS, P, 2 * KD, RANK)
    b_gu = np.stack([padded(a[f"L0_cond_B_{n}"][0], 1).reshape(ADAPTERS, FC, P, RANK) for n in ("gate", "up")], 3)
    b_gu = b_gu.transpose(0, 1, 4, 3, 2).reshape(ADAPTERS, FC, RANK, 2 * P)
    a_dn = padded(a["L0_cond_A_down"][0], 2).reshape(ADAPTERS, RANK, FC, P).transpose(0, 3, 2, 1)
    b_dn = a["L0_cond_B_down"][0].transpose(0, 2, 1)
    q_w = np.ascontiguousarray(tiles(a["L0_ffn_quantized_weights"])).view(np.int32)
    blocks = D // 64
    q_scale = np.repeat(a["L0_ffn_scale_values"].reshape(D, blocks).T, 64, 0).reshape(KD, P, D).transpose(1, 0, 2)
    routers = np.stack([tiles(a["L1_cond_Wr"]), tiles(a["L1_ffn_W_router"])], 1)
    l1_w = np.stack([np.concatenate([tiles(a[w]).reshape(P, -1), tiles(a[la].reshape(E * RANK, D)).reshape(P, -1),
                                     a[lb].transpose(0, 2, 1).reshape(P, D)], 1)
                     for w, la, lb in (("L1_cond_W", "L1_cond_A", "L1_cond_B"), ("L1_ffn_W_base", "L1_ffn_A", "L1_ffn_B"))])
    ids = np.stack([a["itok_B_2_6"], a["itok_B_0_7"]])

    nc = _bacc.Bacc("TRN2", target_bir_lowering=False, num_devices=1)
    arrays, args = {}, []
    for name, v in (("x", x), ("ids", ids), ("consts", consts), ("a_gu", a_gu), ("b_gu", b_gu), ("a_dn", a_dn), ("b_dn", b_dn),
                    ("w_ffn", w_ffn), ("q_w", q_w), ("q_scale", q_scale), ("routers", routers), ("l1_w", l1_w)):
        v = np.ascontiguousarray(v)
        arrays[f"in_{name}"] = v
        args.append(nc.dram_tensor(f"in_{name}", v.shape, mybir.dt.from_np(v.dtype), kind="ExternalInput").ap())
    args.append(nc.dram_tensor("out_t", (HALVES, P, KD, TOK), F32, kind="ExternalOutput").ap())
    build(nc, *args)
    r = _run(nc, [arrays], core_ids=[0])
    o = np.asarray(r.results[0]["out_t"])
    return np.ascontiguousarray(o.transpose(0, 3, 2, 1)).reshape(B, P, D)
```

```python
from contextlib import ExitStack

import concourse.bass as bass
from concourse import mybir

F32 = mybir.dt.float32
F32R = mybir.dt.float32r
I32 = mybir.dt.int32
I8 = mybir.dt.int8
U32 = mybir.dt.uint32
ALU = mybir.AluOpType
ACT = mybir.ActivationFunctionType

P = 128
B = 8
D = 512
KD = D // P
HALVES = 2
HS = B // HALVES
TOK = HS * P
F = 1376
FC = -(-F // P)
RANK = 16
ADAPTERS = 16
E = 8
PAIR = 2 * RANK
GU = 2 * KD * P
AG = 2 * KD * RANK
LW = KD * D + KD * P + D
LORA_SCALE = 0.5
LANG_BIAS = 5.0
STEPS = HALVES * FC
LOOPED = 4
RC = PAIR + E
C_PAIR, C_DOWN, C_ID, C_IOTA, C_BIAS = 0, 256, 768, 896, 904
CONSTS = 912


def build(nc, x, ids, consts, a_sel, b_gu, b_dn, w_ffn, q_w, q_scale, routers, l1_w, out):
    with ExitStack() as ctx:
        def sem(name):
            return ctx.enter_context(nc.semaphore(name))

        def sb(name, shape, dt=F32, where=ctx):
            return where.enter_context(nc.sbuf_tensor(name, shape, dt))

        ids_sb = sb("ids_sb", [1, 8], I32)
        lang_i = sb("lang_i", [P, B], I32)
        lang_f = sb("lang_f", [P, B])
        cst = sb("cst", [P, CONSTS])
        XF = sb("XF", [P, KD, HALVES * TOK])
        PH = sb("PH", [P, KD, HALVES * TOK], F32R)
        PL = sb("PL", [P, KD, HALVES * TOK], F32R)
        l1_raw = sb("l1_raw", [P, LW])
        q_i32 = sb("q_i32", [P, KD, D // 4], I32)
        q_sc = sb("q_sc", [P, KD, D])
        q_f = sb("q_f", [P, D])
        QH = sb("QH", [P, KD, D], F32R)
        QL = sb("QL", [P, KD, D], F32R)
        rt_raw = sb("rt_raw", [P, 2, KD, E])
        RT = sb("RT", [P, 2, KD, RC], F32R)
        warm = sb("warm", [P, 1])
        lang_bias = sb("lang_bias", [P, B, E])
        pair_mask = cst[:, C_PAIR:C_PAIR + 256]
        down_mask = cst[:, C_DOWN:C_DOWN + TOK]
        ident = cst[:, C_ID:C_ID + P]
        iota_e = cst[:, C_IOTA:C_IOTA + E]

        early = ctx.enter_context(ExitStack())
        w_raw = [sb(f"w_raw{i}", [P, GU + D], where=early) for i in range(2)]
        GUH = [sb(f"GUH{i}", [P, 2, KD, P], F32R, early) for i in range(2)]
        GUL = [sb(f"GUL{i}", [P, 2, KD, P], F32R, early) for i in range(2)]
        WDH = [sb(f"WDH{i}", [P, D], F32R, early) for i in range(2)]
        WDL = [sb(f"WDL{i}", [P, D], F32R, early) for i in range(2)]
        b_raw = [sb(f"b_raw{i}", [PAIR, 2, 2 * P], where=early) for i in range(2)]
        BGU = [sb(f"BGU{i}", [3 * PAIR, 2, 2 * P], F32R, early) for i in range(2)]
        sel_raw = sb("sel_raw", [P, B, AG + FC * RANK], where=early)
        a_raw = sel_raw[:, :, 0:AG].rearrange("p b (k r) -> p b k r", r=RANK)
        ad_raw = sel_raw[:, :, AG:].rearrange("p b (c r) -> p b c r", r=RANK)
        ADN = [sb(f"ADN{i}", [P, 2, HS * RANK], F32R, early) for i in range(2)]
        bd_raw = sb("bd_raw", [HS * RANK, HALVES, D], where=early)
        BD1 = sb("BD1", [P, HALVES, D], F32R, early)
        BD2 = sb("BD2", [P, HALVES, D], F32R, early)
        AH = sb("AH", [P, HALVES, 2 * KD, HS, RANK], F32R, early)
        AL = sb("AL", [P, HALVES, 2 * KD, HS, RANK], F32R, early)
        TM = sb("TM", [P, TOK], where=early)
        TH = sb("TH", [P, TOK], F32R, early)
        TL = sb("TL", [P, TOK], F32R, early)
        RGU = sb("RGU", [3 * PAIR, HALVES, 2, 2, 2 * P], F32R, early)
        TDM = sb("TDM", [P, TOK], where=early)
        TD1 = sb("TD1", [P, TOK], F32R, early)
        TD2 = sb("TD2", [P, TOK], F32R, early)
        sil = [sb(f"sil{i}", [P, TOK], where=early) for i in range(2)]
        act_f = [sb(f"act_f{i}", [P, TOK], where=early) for i in range(2)]
        ACH = [sb(f"ACH{i}", [P, TOK], F32R, early) for i in range(2)]
        ACL = [sb(f"ACL{i}", [P, TOK], F32R, early) for i in range(2)]
        early.close()

        UH = sb("UH", [P, KD, HALVES * TOK], F32R)
        UL = sb("UL", [P, KD, HALVES * TOK], F32R)
        LH = [sb(f"LH{i}", [P, LW], F32R) for i in range(2)]
        LL = [sb(f"LL{i}", [P, LW], F32R) for i in range(2)]
        hid = sb("hid", [P, TOK])
        gh = sb("gh", [P, TOK])
        GHH = sb("GHH", [P, TOK], F32R)
        GHL = sb("GHL", [P, TOK], F32R)
        route_t = sb("route_t", [RC, TOK])
        part_l = sb("part_l", [P, HS, E])
        logit = sb("logit", [P, HS, E])
        top8 = sb("top8", [P, HS, E])
        top8_i = sb("top8_i", [P, HS, E], U32)
        top2_f = sb("top2_f", [P, HS, 2])
        gap = sb("gap", [P, HS, 1])
        gap_e = sb("gap_e", [P, HS, 1])
        half_sum = sb("half_sum", [P, HS, 1])
        gate2 = sb("gate2", [P, HS, 2])
        onehot = sb("onehot", [P, HS, 2, E])
        chosen = sb("chosen", [P, HS, 2, E])
        gates = sb("gates", [P, HS, E])
        gates_r = sb("gates_r", [P, HS, E, RANK])

        PB = [ctx.enter_context(nc.psum_tensor(f"bank{i}", [P, TOK], F32)) for i in range(8)]
        GATE, UP, TDN, TGU = PB[4], PB[5], PB[6], PB[7]
        ROUTE, HID, GATET, LOGITS = PB[4:8]

        ids_in, x_in, cst_in, lang_in = sem("ids_in"), [sem(f"x_in{k}") for k in range(KD + 1)], sem("cst_in"), sem("lang_in")
        a_in, bd_in, q_in, rt_in, gu0_in = [sem("a_in0"), sem("a_in1")], sem("bd_in"), sem("q_in"), sem("rt_in"), sem("gu0_in")
        w_in, b_in = [sem("w_in0"), sem("w_in1")], [sem("b_in0"), sem("b_in1")]
        first_w_in = [sem("first_w_in0"), sem("first_w_in1")]
        l1_in = [sem("l1_in0"), sem("l1_in1")]
        x_hi, x_split = sem("x_hi"), sem("x_split")
        a_hi, a_split = sem("a_hi"), sem("a_split")
        gu0_hi, gu0_split, warm_zero = sem("gu0_hi"), sem("gu0_split"), sem("warm_zero")
        gu_hi, gu_split, b_hi, b_split = sem("gu_hi"), sem("gu_split"), sem("b_hi"), sem("b_split")
        dn_hi, dn_split = sem("dn_hi"), sem("dn_split")
        bd_hi, bd_split = sem("bd_hi"), sem("bd_split")
        t_done, t_masked, t_hi, t_rest, r_hi, r_rest = (sem(n) for n in ("t_done", "t_masked", "t_hi", "t_rest", "r_hi", "r_rest"))
        gu_done, silu_done, act_done, act_hi, act_split = (sem(n) for n in ("gu_done", "silu_done", "act_done", "act_hi", "act_split"))
        dn_done, td_done, td_masked, td_hi, td_split, td_shift = (sem(n) for n in ("dn_done", "td_done", "td_masked", "td_hi", "td_split", "td_shift"))
        d_done, d_hi, d_split = sem("d_done"), sem("d_hi"), sem("d_split")
        q_prod, q_hi, q_split, rt_zero, rt_hi, rt_split = (sem(n) for n in ("q_prod", "q_hi", "q_split", "rt_zero", "rt_hi", "rt_split"))
        f_done, x2_done, u_hi, u_split = (sem(n) for n in ("f_done", "x2_done", "u_hi", "u_split"))
        l1_hi, l1_split = sem("l1_hi"), sem("l1_split")
        route_done, route_copied, logits_done, gap_done, exp_done, gates_done = (sem(n) for n in ("route_done", "route_copied", "logits_done", "gap_done", "exp_done", "gates_done"))
        hid_done, hid_copied, gatet_done, gh_done, gh_hi, gh_split = (sem(n) for n in ("hid_done", "hid_copied", "gatet_done", "gh_done", "gh_hi", "gh_split"))
        o_done, y_hi, y_split, x3_done, stored = (sem(n) for n in ("o_done", "y_hi", "y_split", "x3_done", "stored"))
        chain = sem("chain")

        def half(h):
            return slice(h * TOK, (h + 1) * TOK)

        def f32(ap):
            return ap.bitcast(F32)

        def gate_bank(s):
            return PB[0] if isinstance(s, int) and s == 1 else GATE

        def up_bank(s):
            return PB[1] if isinstance(s, int) and s == 1 else UP

        def dyn(i):
            return bass.DynSlice(i, 1)

        def steps(eng, h, step, first=2, turns=LOOPED):
            with eng.Fori(0, turns) as i:
                for j in range(2):
                    k = h * FC + first + j
                    step(i * 2 + (first + j), i * 2 + k, k % 2, i + k // 2)

        def one_step(h, c, step):
            s = h * FC + c
            step(c, s, s % 2, s // 2)

        block = ctx.enter_context(nc.Block())

        @block.sync
        def _(sp):
            sp.dma_start(ids_sb[:, :], ids[0:1, :]).then_inc(ids_in, 16)
            sp.dma_start(w_raw[0][:, 0:GU], w_ffn[0, :, 0:GU]).then_inc(gu0_in, 16)
            for k in range(KD):
                sp.dma_start(XF[:, k, half(0)], x[0, :, k, :]).then_inc(x_in[k], 16)
            sp.wait_ge(ids_in, 16)
            who = {}

            def load_b(c, par, h):
                for i in range(HS):
                    sp.dma_start(b_raw[par][RANK * (i % 2):RANK * (i % 2) + RANK, i // 2, :],
                                 b_gu[dyn(who[h * HS + i]), c].rearrange("a c r n -> r (a c n)")).then_inc(b_in[par], 16)

            for h in range(HALVES):
                mine = range(h * HS, (h + 1) * HS)
                for b in mine:
                    who[b] = sp.value_load(ids_sb[0:1, b:b + 1], min_val=0, max_val=ADAPTERS - 1)
                for b in mine:
                    sp.dma_start(sel_raw[:, b:b + 1, :], a_sel[dyn(who[b])].rearrange("a p n -> p a n")).then_inc(a_in[h], 16)
                if h == 0:
                    load_b(slice(0, 1), 0, 0)
                    load_b(slice(1, 2), 1, 0)
            for b in range(B):
                sp.dma_start(bd_raw[RANK * (b % HS):RANK * (b % HS) + RANK, b // HS, :],
                             b_dn[dyn(who[b])].rearrange("a r n -> r (a n)")).then_inc(bd_in, 16)

            def load(h):
                def step(c, s, par, turn):
                    sp.wait_ge(dn_split, s - 1)
                    sp.dma_start(w_raw[par][:, :], w_ffn[dyn(c)].rearrange("a p n -> p (a n)")).then_inc(w_in[par], 16)
                    sp.wait_ge(b_split, s - 1)
                    load_b(dyn(c), par, h)
                return step

            steps(sp, 0, load(0))
            one_step(0, FC - 1, load(0))
            sp.dma_start(q_i32[:, :, :], q_w[:, :, :]).then_inc(q_in, 16)
            sp.dma_start(q_sc[:, :, :], q_scale[:, :, :]).then_inc(q_in, 16)
            sp.dma_start(rt_raw[:, :, :, :], routers[:, :, :, :]).then_inc(rt_in, 16)
            sp.dma_start(l1_raw[:, :], l1_w[0]).then_inc(l1_in[0], 16)
            steps(sp, 1, load(1), first=0, turns=LOOPED + 1)
            one_step(1, FC - 1, load(1))
            sp.wait_ge(l1_split, 4)
            sp.dma_start(l1_raw[:, :], l1_w[1]).then_inc(l1_in[1], 16)
            for h in range(HALVES):
                for o in range(KD):
                    sp.wait_ge(x3_done, h * KD + o + 1)
                    sp.dma_start(out[h, :, o, :], XF[:, o, half(h)]).then_inc(stored, 16)
            sp.wait_ge(stored, 16 * HALVES * KD)

        @block.gpsimd
        def _(pool):
            nc.gpsimd.memset(warm[:, :], 0.0).then_inc(warm_zero, 1)
            nc.gpsimd.memset(f32(RT[:, :, :, :]), 0.0).then_inc(rt_zero, 1)
            pool.wait_ge(x_in[KD - 1], 16)
            pool.dma_start(w_raw[1][:, :], w_ffn[1]).then_inc(first_w_in[1], 16)
            pool.dma_start(cst[:, :], consts[:, :]).then_inc(cst_in, 16)
            pool.dma_start(w_raw[0][:, GU:GU + D], w_ffn[0, :, GU:GU + D]).then_inc(first_w_in[0], 16)
            pool.dma_start(XF[:, :, half(1)], x[1]).then_inc(x_in[KD], 16)
            pool.dma_start(lang_i[:, :], ids[1:2, :].partition_broadcast(P)).then_inc(lang_in, 16)

        @block.scalar
        def _(act):
            def high(dst, src):
                return nc.scalar.activation(dst, src, ACT.Copy)

            act.wait_ge(warm_zero, 1)
            nc.scalar.activation(warm[:, :], warm[:, :], ACT.Silu)

            def split_x(h, ks=range(KD)):
                for k in ks:
                    act.wait_ge(x_in[KD if h else k], 16)
                    high(PH[:, k, half(h)], XF[:, k, half(h)]).then_inc(x_hi, 1)

            def split_a(h):
                act.wait_ge(a_in[h], 16 * HS)
                high(AH[:, h].rearrange("p k b r -> p b k r"), a_raw[:, h * HS:(h + 1) * HS]).then_inc(a_hi, 1)

            def split_gu(par):
                high(GUH[par][:, :, :, :].rearrange("p g k m -> p (g k m)"), w_raw[par][:, 0:GU]).then_inc(gu_hi, 1)

            def split_b(s, par, turn):
                act.wait_ge(b_in[par], (turn + 1) * 16 * HS)
                high(BGU[par][0:PAIR, :, :], b_raw[par][:, :, :])
                high(BGU[par][PAIR:2 * PAIR, :, :], b_raw[par][:, :, :]).then_inc(b_hi, 1)

            def rhs_gu(h):
                act.wait_ge(t_masked, h + 1)
                if h:
                    act.wait_ge(r_hi, h)
                high(TH[:, :], TM[:, :]).then_inc(t_hi, 1)
                if h == 0:
                    split_x(1)
                act.wait_ge(t_rest, h + 1)
                for g in range(2):
                    for p in range(2):
                        q = PAIR * (2 * g + p)
                        last = high(RGU[PAIR:2 * PAIR, h, p, g, :], f32(TL[q:q + PAIR, 2 * P * p:2 * P * p + 2 * P]))
                last.then_inc(r_rest, 1)

            def weights_in(s, par, turn):
                if isinstance(s, int) and s < 2:
                    act.wait_ge(first_w_in[par], 16)
                else:
                    act.wait_ge(w_in[par], turn * 16)

            def split_down(h, c, s, par, turn):
                if not isinstance(s, int) or s >= 2:
                    act.wait_ge(dn_done, s - 1)
                weights_in(s, par, turn)
                cs = slice(c, c + 1) if isinstance(c, int) else dyn(c)
                high(ADN[par][:, 0, :].rearrange("p (b r) -> p b r", r=RANK),
                     ad_raw[:, h * HS:(h + 1) * HS, cs, :].rearrange("p b c r -> p b (c r)"))
                high(WDH[par][:, :], w_raw[par][:, GU:GU + D]).then_inc(dn_hi, 1)

            def step_for(h):
                def step(c, s, par, turn, more=True):
                    if not isinstance(s, int) or s > 0:
                        split_down(h, c, s, par, turn)
                    if more:
                        nxt, nturn = 1 - par, turn + par
                        weights_in(s + 1, nxt, nturn)
                        if not isinstance(s, int) or s >= 1:
                            act.wait_ge(gu_done, s)
                        split_gu(nxt)
                        split_b(s + 1, nxt, nturn)
                    act.wait_ge(gu_done, s + 1)
                    nc.scalar.activation(sil[par][:, :], gate_bank(s)[:, :], ACT.Silu).then_inc(silu_done, 1)
                    act.wait_ge(act_done, s + 1)
                    high(ACH[par][:, :], act_f[par][:, :]).then_inc(act_hi, 1)
                return step

            def down_rhs(h):
                act.wait_ge(td_masked, h + 1)
                high(TD1[:, :], TDM[:, :]).then_inc(td_hi, 1)
                high(TD2[64:128, :], TDM[0:64, :]).then_inc(td_shift, 1)

            def cond_out(h):
                for o in range(KD):
                    act.wait_ge(d_done, h * KD + o + 1)
                    high(PH[:, o, half(h)], PB[o][:, :]).then_inc(d_hi, 1)

            def split_q(ks):
                for k in ks:
                    act.wait_ge(q_prod, k + 1)
                    high(QH[:, k, :], q_f[:, :]).then_inc(q_hi, 1)

            act.wait_ge(gu0_in, 16)
            high(GUH[0][:, 0], w_raw[0][:, 0:GU // 2].rearrange("p (k m) -> p k m", k=KD)).then_inc(gu0_hi, 1)
            split_x(0, range(0, 1))
            high(GUH[0][:, 1], w_raw[0][:, GU // 2:GU].rearrange("p (k m) -> p k m", k=KD)).then_inc(gu0_hi, 1)
            split_x(0, range(1, KD))
            split_a(0)
            weights_in(1, 1, 0)
            split_gu(1)
            split_b(0, 0, 0)
            split_b(1, 1, 0)
            one_step(0, 0, lambda *a: split_down(0, *a))
            split_a(1)
            rhs_gu(0)
            one_step(0, 0, lambda *a: step_for(0)(*a, more=False))
            one_step(0, 1, step_for(0))
            rhs_gu(1)
            steps(act, 0, step_for(0))
            act.wait_ge(bd_in, 16 * B)
            high(BD1[0:64, :, :], bd_raw[:, :, :])
            high(BD1[64:128, :, :], bd_raw[:, :, :])
            high(BD2[0:64, :, :], bd_raw[:, :, :]).then_inc(bd_hi, 1)
            one_step(0, FC - 1, step_for(0))
            down_rhs(0)
            one_step(1, 0, step_for(1))
            cond_out(0)
            one_step(1, 1, step_for(1))
            act.wait_ge(rt_in, 16)
            act.wait_ge(rt_zero, 1)
            for i in range(2):
                high(RT[:, i, :, 0:E], rt_raw[:, i, :, :]).then_inc(rt_hi, 1)
            split_q(range(0, 2))
            steps(act, 1, step_for(1))
            split_q(range(2, KD))
            one_step(1, FC - 1, lambda *a: step_for(1)(*a, more=False))
            down_rhs(1)

            def split_l1(i, q):
                n = LW // 4
                if q == 0:
                    act.wait_ge(l1_in[i], 16)
                high(LH[i][:, q * n:(q + 1) * n], l1_raw[:, q * n:(q + 1) * n]).then_inc(l1_hi, 1)

            def split_x2(t):
                h, o = divmod(t, KD)
                act.wait_ge(x2_done, t + 1)
                high(UH[:, o, half(h)], XF[:, o, half(h)]).then_inc(u_hi, 1)

            split_x2(0)
            split_x2(1)
            cond_out(1)
            for t in range(2, HALVES * KD):
                split_x2(t)
                if t < 6:
                    split_l1(0, t - 2)
            for i in range(2):
                for h in range(HALVES):
                    n = 2 * i + h
                    act.wait_ge(route_done, n + 1)
                    nc.scalar.activation(route_t[:, :], ROUTE[0:RC, :], ACT.Copy).then_inc(route_copied, 1)
                    act.wait_ge(gap_done, n + 1)
                    nc.scalar.activation(gap_e[:, :, :], gap[:, :, :], ACT.Exp).then_inc(exp_done, 1)
                    act.wait_ge(hid_done, n + 1)
                    if n:
                        act.wait_ge(gh_done, n)
                    nc.scalar.activation(hid[:, :], HID[:, :], ACT.Copy).then_inc(hid_copied, 1)
                    if n == 0:
                        split_l1(1, 0)
                        split_l1(1, 1)
                    act.wait_ge(gh_done, n + 1)
                    high(GHH[:, :], gh[:, :]).then_inc(gh_hi, 1)
                    if n == 0:
                        split_l1(1, 2)
                        split_l1(1, 3)
                    for o in range(KD):
                        if i == 0:
                            act.wait_ge(o_done, n * KD + o + 1)
                            high(PH[:, o, half(h)], PB[o][:, :]).then_inc(y_hi, 1)

        @block.vector
        def _(dve):
            count = [0]

            def link(ins):
                count[0] += 1
                ins.then_inc(chain, 1)
                dve.wait_ge(chain, count[0])

            def rest(dst, src, hi):
                return nc.vector.tensor_tensor(dst, src, f32(hi), ALU.subtract)

            def split_x(h, ks=range(KD)):
                for k in ks:
                    dve.wait_ge(x_hi, h * KD + k + 1)
                    rest(PL[:, k, half(h)], XF[:, k, half(h)], PH[:, k, half(h)]).then_inc(x_split, 1)

            def split_b(s, par):
                dve.wait_ge(b_hi, s + 1)
                rest(BGU[par][2 * PAIR:3 * PAIR, :, :], b_raw[par][:, :, :], BGU[par][0:PAIR, :, :]).then_inc(b_split, 1)

            def rhs_gu(h):
                dve.wait_ge(t_done, h + 1)
                if h:
                    dve.wait_ge(t_hi, h)
                nc.vector.tensor_tensor(TM[:, :].rearrange("p (a n) -> p a n", a=2),
                                        TGU[:, :].rearrange("p (a n) -> p a n", a=2),
                                        pair_mask.unsqueeze(1).to_broadcast([P, 2, 256]), ALU.mult).then_inc(t_masked, 1)
                dve.wait_ge(t_hi, h + 1)
                if h:
                    dve.wait_ge(r_rest, h)
                rest(TL[:, :], TM[:, :], TH[:, :]).then_inc(t_rest, 1)
                for g in range(2):
                    for p in range(2):
                        q = PAIR * (2 * g + p)
                        for row in (0, 2 * PAIR):
                            last = nc.vector.tensor_copy(RGU[row:row + PAIR, h, p, g, :],
                                                         TH[q:q + PAIR, 2 * P * p:2 * P * p + 2 * P])
                last.then_inc(r_hi, 1)

            def split_gu(s, par):
                dve.wait_ge(gu_hi, s)
                rest(GUL[par][:, :, :, :].rearrange("p g k m -> p (g k m)"), w_raw[par][:, 0:GU],
                     GUH[par][:, :, :, :].rearrange("p g k m -> p (g k m)")).then_inc(gu_split, 1)

            def split_down(h, c, s, par):
                dve.wait_ge(dn_hi, s + 1)
                cs = slice(c, c + 1) if isinstance(c, int) else dyn(c)
                rest(ADN[par][:, 1, :].rearrange("p (b r) -> p b r", r=RANK),
                     ad_raw[:, h * HS:(h + 1) * HS, cs, :].rearrange("p b c r -> p b (c r)"),
                     ADN[par][:, 0, :].rearrange("p (b r) -> p b r", r=RANK))
                rest(WDL[par][:, :], w_raw[par][:, GU:GU + D], WDH[par][:, :]).then_inc(dn_split, 1)

            def step_for(h):
                def step(c, s, par, turn, more=True):
                    if not isinstance(s, int) or s > 0:
                        split_down(h, c, s, par)
                    if more:
                        split_gu(s + 1, 1 - par)
                        split_b(s + 1, 1 - par)
                    dve.wait_ge(silu_done, s + 1)
                    nc.vector.tensor_tensor(act_f[par][:, :], sil[par][:, :], up_bank(s)[:, :], ALU.mult).then_inc(act_done, 1)
                    dve.wait_ge(act_hi, s + 1)
                    rest(ACL[par][:, :], act_f[par][:, :], ACH[par][:, :]).then_inc(act_split, 1)
                return step
            def down_rhs(h):
                dve.wait_ge(td_done, h + 1)
                nc.vector.tensor_tensor(TDM[:, :], TDN[:, :], down_mask, ALU.mult).then_inc(td_masked, 1)
                dve.wait_ge(td_hi, h + 1)
                rest(TD2[0:64, :], TDM[0:64, :], TD1[0:64, :]).then_inc(td_split, 1)

            def cond_out(h):
                for o in range(KD):
                    dve.wait_ge(d_hi, h * KD + o + 1)
                    rest(PL[:, o, half(h)], PB[o][:, :], PH[:, o, half(h)]).then_inc(d_split, 1)

            def split_q(ks):
                for k in ks:
                    if k:
                        dve.wait_ge(q_split, k)
                    else:
                        dve.wait_ge(q_in, 32)
                    nc.vector.tensor_tensor(q_f[:, :], q_i32[:, k, :].bitcast(I8), q_sc[:, k, :], ALU.mult).then_inc(q_prod, 1)
                    dve.wait_ge(q_hi, k + 1)
                    rest(QL[:, k, :], q_f[:, :], QH[:, k, :]).then_inc(q_split, 1)

            def split_gu0(g):
                dve.wait_ge(gu0_hi, g + 1)
                rest(GUL[0][:, g], w_raw[0][:, g * GU // 2:(g + 1) * GU // 2].rearrange("p (k m) -> p k m", k=KD), GUH[0][:, g]).then_inc(gu0_split, 1)

            split_gu0(0)
            split_x(0, range(0, 1))
            split_gu0(1)
            split_x(0, range(1, KD))
            def split_a(h):
                dve.wait_ge(a_hi, h + 1)
                rest(AL[:, h].rearrange("p k b r -> p b k r"), a_raw[:, h * HS:(h + 1) * HS],
                     AH[:, h].rearrange("p k b r -> p b k r")).then_inc(a_split, 1)

            split_a(0)
            split_gu(1, 1)
            split_b(0, 0)
            split_b(1, 1)
            split_down(0, 0, 0, 0)
            split_a(1)
            dve.wait_ge(cst_in, 16)
            rhs_gu(0)
            split_x(1)
            one_step(0, 0, lambda *a: step_for(0)(*a, more=False))
            one_step(0, 1, step_for(0))
            rhs_gu(1)
            steps(dve, 0, step_for(0))
            dve.wait_ge(bd_hi, 1)
            rest(BD2[64:128, :, :], bd_raw[:, :, :], BD1[0:64, :, :]).then_inc(bd_split, 1)
            one_step(0, FC - 1, step_for(0))
            down_rhs(0)
            one_step(1, 0, step_for(1))
            cond_out(0)
            one_step(1, 1, step_for(1))
            for i in range(2):
                dve.wait_ge(rt_hi, i + 1)
                rest(RT[:, i, :, PAIR:RC], rt_raw[:, i, :, :], RT[:, i, :, 0:E]).then_inc(rt_split, 1)
            split_q(range(0, 2))
            dve.wait_ge(lang_in, 16)
            link(nc.vector.tensor_copy(lang_f[:, :], lang_i[:, :]))
            link(nc.vector.tensor_tensor(lang_bias[:, :, :], iota_e.unsqueeze(1).to_broadcast([P, B, E]),
                                         lang_f[:, :].unsqueeze(2).to_broadcast([P, B, E]), ALU.is_equal))
            link(nc.vector.tensor_scalar(lang_bias[:, :, :], lang_bias[:, :, :], LANG_BIAS, None, ALU.mult))
            steps(dve, 1, step_for(1))
            split_q(range(2, KD))
            one_step(1, FC - 1, lambda *a: step_for(1)(*a, more=False))
            down_rhs(1)

            def split_l1(i, q):
                n = LW // 4
                dve.wait_ge(l1_hi, 4 * i + q + 1)
                rest(LL[i][:, q * n:(q + 1) * n], l1_raw[:, q * n:(q + 1) * n], LH[i][:, q * n:(q + 1) * n]).then_inc(l1_split, 1)

            def x2_tile(t):
                h, o = divmod(t, KD)
                dve.wait_ge(f_done, t + 1)
                nc.vector.scalar_tensor_tensor(XF[:, o, half(h)], PB[o if h else o + 4][:, :], cst[:, C_BIAS + o:C_BIAS + o + 1],
                                               XF[:, o, half(h)], ALU.add, ALU.add).then_inc(x2_done, 1)
                dve.wait_ge(u_hi, t + 1)
                rest(UL[:, o, half(h)], XF[:, o, half(h)], UH[:, o, half(h)]).then_inc(u_split, 1)

            x2_tile(0)
            x2_tile(1)
            cond_out(1)
            for t in range(2, HALVES * KD):
                x2_tile(t)
                if t < 6:
                    split_l1(0, t - 2)
            for i in range(2):
                for h in range(HALVES):
                    n = 2 * i + h
                    dve.wait_ge(logits_done, n + 1)
                    route = LOGITS[:, 0:HS * RC].rearrange("p (j c) -> p j c", c=RC)
                    if i == 0:
                        link(nc.vector.tensor_tensor(part_l[:, :, :], route[:, :, 0:E], lang_bias[:, h * HS:(h + 1) * HS, :], ALU.add))
                    else:
                        link(nc.vector.tensor_copy(part_l[:, :, :], route[:, :, 0:E]))
                    link(nc.vector.tensor_tensor(logit[:, :, :], part_l[:, :, :], route[:, :, PAIR:RC], ALU.add))
                    for j in range(HS):
                        last = nc.vector.max(top8[:, j, :], logit[:, j, :])
                    link(last)
                    nc.vector.tensor_tensor(gap[:, :, :], top8[:, :, 1:2], top8[:, :, 0:1], ALU.subtract).then_inc(gap_done, 1)
                    for j in range(HS):
                        last = nc.vector.max_index(top8_i[:, j, :], top8[:, j, :], logit[:, j, :])
                    link(last)
                    link(nc.vector.tensor_copy(top2_f[:, :, :], top8_i[:, :, 0:2]))
                    nc.vector.tensor_tensor(onehot[:, :, :, :], cst[:, C_IOTA:C_IOTA + E].unsqueeze(1).unsqueeze(1).to_broadcast([P, HS, 2, E]),
                                            top2_f[:, :, :].unsqueeze(3).to_broadcast([P, HS, 2, E]), ALU.is_equal)
                    dve.wait_ge(exp_done, n + 1)
                    link(nc.vector.tensor_scalar(half_sum[:, :, :], gap_e[:, :, :], 0.5, 0.5, ALU.mult, ALU.add))
                    link(nc.vector.reciprocal(gate2[:, :, 0:1], half_sum[:, :, :]))
                    link(nc.vector.tensor_tensor(gate2[:, :, 1:2], gate2[:, :, 0:1], gap_e[:, :, :], ALU.mult))
                    link(nc.vector.tensor_tensor(chosen[:, :, :, :], onehot[:, :, :, :], gate2[:, :, :].unsqueeze(3).to_broadcast([P, HS, 2, E]), ALU.mult))
                    link(nc.vector.tensor_tensor(gates[:, :, :], chosen[:, :, 0, :], chosen[:, :, 1, :], ALU.add))
                    nc.vector.tensor_copy(gates_r[:, :, :, :], gates[:, :, :].unsqueeze(3).to_broadcast([P, HS, E, RANK])).then_inc(gates_done, 1)
                    dve.wait_ge(gatet_done, n + 1)
                    dve.wait_ge(hid_copied, n + 1)
                    nc.vector.tensor_tensor(gh[:, :], hid[:, :], GATET[:, :], ALU.mult).then_inc(gh_done, 1)
                    dve.wait_ge(gh_hi, n + 1)
                    rest(GHL[:, :], gh[:, :], GHH[:, :]).then_inc(gh_split, 1)
                    if n == 0:
                        for q in range(4):
                            split_l1(1, q)
                    for o in range(KD):
                        if i == 0:
                            dve.wait_ge(y_hi, n * KD + o + 1)
                            rest(PL[:, o, half(h)], PB[o][:, :], PH[:, o, half(h)]).then_inc(y_split, 1)
                        else:
                            dve.wait_ge(o_done, n * KD + o + 1)
                            nc.vector.scalar_tensor_tensor(XF[:, o, half(h)], PB[o][:, :], cst[:, C_BIAS + KD + o:C_BIAS + KD + o + 1],
                                                           XF[:, o, half(h)], ALU.add, ALU.add).then_inc(x3_done, 1)

        @block.tensor
        def _(pe):
            def product(bank, wh, wl, mh, ml, start, stop):
                nc.tensor.matmul(bank, wh, mh, start=start, stop=False)
                nc.tensor.matmul(bank, wh, ml, start=False, stop=False)
                return nc.tensor.matmul(bank, wl, mh, start=False, stop=stop)

            def t_gu(h):
                pe.wait_ge(a_split, h + 1)
                pe.wait_ge(x_split, (h + 1) * KD)
                if h:
                    pe.wait_ge(t_masked, h)
                for k in range(KD):
                    cols = [t[:, h].rearrange("p k b r -> p k (b r)")[:, 2 * k:2 * k + 2, :] for t in (AH, AL)]
                    last = product(TGU[:, :], cols[0].rearrange("p g m -> p (g m)"), cols[1].rearrange("p g m -> p (g m)"),
                                   PH[:, k, half(h)], PL[:, k, half(h)], k == 0, k == KD - 1)
                last.then_inc(t_done, 1)

            def main_k(h, par, g, bank, k):
                product(bank[:, :], GUH[par][:, g, k, :], GUL[par][:, g, k, :], PH[:, k, half(h)], PL[:, k, half(h)], k == 0, k == KD - 1)

            def gate_up_main(h):
                def step(c, s, par, turn):
                    pe.wait_ge(gu_split, s)
                    if isinstance(c, int) and c == 0:
                        pe.wait_ge(x_split, (h + 1) * KD)
                    for g, bank in enumerate((gate_bank(s), up_bank(s))):
                        if not isinstance(s, int) or s > 1:
                            pe.wait_ge((silu_done, act_done)[g], s)
                        for k in range(KD):
                            main_k(h, par, g, bank, k)
                return step

            def gate_up_lora(h):
                def step(c, s, par, turn):
                    pe.wait_ge(b_split, s + 1)
                    if isinstance(c, int) and c == 0:
                        pe.wait_ge(r_hi, h + 1)
                        pe.wait_ge(r_rest, h + 1)
                    for g, bank in enumerate((gate_bank(s), up_bank(s))):
                        for p in range(2):
                            last = nc.tensor.matmul(bank[:, 2 * P * p:2 * P * p + 2 * P], BGU[par][:, p, g * P:(g + 1) * P],
                                                    RGU[:, h, p, g, :], start=False, stop=True, skip_group_check=True)
                    last.then_inc(gu_done, 1)
                return step

            def down_a(h):
                def step(c, s, par, turn):
                    first = isinstance(c, int) and c == 0
                    final = isinstance(c, int) and c == FC - 1
                    pe.wait_ge(dn_split, s + 1)
                    pe.wait_ge(act_split, s + 1)
                    if first and h:
                        pe.wait_ge(td_masked, h)
                    nc.tensor.matmul(TDN[:, :], ADN[par][:, :, :].rearrange("p a m -> p (a m)"), ACH[par][:, :], start=first, stop=final, skip_group_check=True)
                    last = nc.tensor.matmul(TDN[0:64, :], ADN[par][:, 0, :], ACL[par][:, :], start=False, stop=final, skip_group_check=True)
                    if final:
                        last.then_inc(td_done, 1)
                return step

            def down_main(h):
                def step(c, s, par, turn):
                    first = isinstance(c, int) and c == 0
                    for o in range(KD):
                        if first and h:
                            pe.wait_ge(d_split, o + 1)
                        elif first and o < 2:
                            pe.wait_ge((silu_done, act_done)[o], 2)
                        m = slice(o * P, (o + 1) * P)
                        last = product(PB[o][:, :], WDH[par][:, m], WDL[par][:, m], ACH[par][:, :], ACL[par][:, :], first, False)
                    last.then_inc(dn_done, 1)
                return step

            def down_lora(h):
                pe.wait_ge(bd_split, 1)
                pe.wait_ge(td_split, h + 1)
                pe.wait_ge(td_shift, h + 1)
                for o in range(KD):
                    m = slice(o * P, (o + 1) * P)
                    nc.tensor.matmul(PB[o][:, :], BD1[:, h, m], TD1[:, :], start=False, stop=False)
                    nc.tensor.matmul(PB[o][:, :], BD2[:, h, m], TD2[:, :], start=False, stop=True).then_inc(d_done, 1)

            def gate_up(h):
                def step(*a):
                    gate_up_main(h)(*a)
                    gate_up_lora(h)(*a)
                return step

            def down(h):
                def step(*a):
                    down_a(h)(*a)
                    down_main(h)(*a)
                return step

            def both(h):
                def step(c, s, par, turn):
                    gate_up(h)(c, s, par, turn)
                    down(h)(c - 1, s - 1, 1 - par, None)
                return step

            def ffn(t):
                h, o = divmod(t, KD)
                if o == 0:
                    pe.wait_ge(q_split, KD)
                    pe.wait_ge(d_split, (h + 1) * KD)
                m = slice(o * P, (o + 1) * P)
                for k in range(KD):
                    last = product(PB[o if h else o + 4][:, :], QH[:, k, m], QL[:, k, m], PH[:, k, half(h)], PL[:, k, half(h)], k == 0, k == KD - 1)
                last.then_inc(f_done, 1)

            for k in range(KD):
                pe.wait_ge(x_split, k + 1)
                for g, bank in enumerate((GATE, UP)):
                    if k == 0:
                        pe.wait_ge(gu0_split, g + 1)
                    main_k(0, 0, g, bank, k)
            t_gu(0)
            one_step(0, 1, gate_up_main(0))
            one_step(0, 0, gate_up_lora(0))
            one_step(0, 1, gate_up_lora(0))
            t_gu(1)
            one_step(0, 0, down(0))
            steps(pe, 0, both(0))
            one_step(0, FC - 1, both(0))
            one_step(0, FC - 1, down_a(0))
            one_step(1, 0, gate_up(1))
            one_step(0, FC - 1, down_main(0))
            down_lora(0)
            one_step(1, 1, both(1))
            steps(pe, 1, both(1))
            one_step(1, FC - 1, both(1))
            one_step(1, FC - 1, down_a(1))
            one_step(1, FC - 1, down_main(1))
            ffn(0)
            ffn(1)
            down_lora(1)
            for t in range(2, HALVES * KD):
                if t == 2:
                    pe.wait_ge(td_masked, 2)
                ffn(t)

            pe.wait_ge(rt_split, 2)
            pe.wait_ge(cst_in, 16)
            for i in range(2):
                WH, WL = (t[:, 0:KD * D].rearrange("p (k n) -> p k n", k=KD) for t in (LH[i], LL[i]))
                AHI, ALO = (t[:, KD * D:KD * D + KD * P].rearrange("p (k n) -> p k n", k=KD) for t in (LH[i], LL[i]))
                BHI, BLO = (t[:, KD * D + KD * P:LW] for t in (LH[i], LL[i]))
                SH, SL = ((UH, UL), (PH, PL))[i]
                for h in range(HALVES):
                    n = 2 * i + h
                    pe.wait_ge((u_split, y_split)[i], (h + 1) * KD)
                    if n:
                        pe.wait_ge(gates_done, n)
                    for k in range(KD):
                        nc.tensor.matmul(ROUTE[0:RC, :], RT[:, i, k, :], SH[:, k, half(h)], start=(k == 0), stop=(k == KD - 1), skip_group_check=True)
                        last = nc.tensor.matmul(ROUTE[0:E, :], RT[:, i, k, 0:E], SL[:, k, half(h)], start=False, stop=(k == KD - 1), skip_group_check=True)
                    last.then_inc(route_done, 1)
                    pe.wait_ge(l1_split, 4 * i + 4)
                    if n:
                        pe.wait_ge(hid_copied, n)
                    for k in range(KD):
                        last = product(HID[:, :], AHI[:, k, :], ALO[:, k, :], SH[:, k, half(h)], SL[:, k, half(h)], k == 0, k == KD - 1)
                    last.then_inc(hid_done, 1)
                    pe.wait_ge(route_copied, n + 1)
                    for j in range(HS):
                        last = nc.tensor.transpose(LOGITS[:, j * RC:(j + 1) * RC], route_t[:, j * P:(j + 1) * P], ident[0:RC, 0:RC])
                    last.then_inc(logits_done, 1)
                    for o in range(KD):
                        m = slice(o * P, (o + 1) * P)
                        if n == 0:
                            pe.wait_ge(x2_done, KD + o + 1)
                        elif n <= 2:
                            pe.wait_ge(y_split, (n - 1) * KD + o + 1)
                        else:
                            pe.wait_ge(x3_done, o + 1)
                        for k in range(KD):
                            product(PB[o][:, :], WH[:, k, m], WL[:, k, m], SH[:, k, half(h)], SL[:, k, half(h)], k == 0, False)
                        if o == 2:
                            pe.wait_ge(gates_done, n + 1)
                            if n:
                                pe.wait_ge(gh_done, n)
                            for j in range(HS):
                                last = nc.tensor.transpose(GATET[:, j * P:(j + 1) * P], gates_r[:, j, :, :].rearrange("p e r -> p (e r)"), ident)
                            last.then_inc(gatet_done, 1)
                    pe.wait_ge(gh_split, n + 1)
                    for o in range(KD):
                        m = slice(o * P, (o + 1) * P)
                        product(PB[o][:, :], BHI[:, m], BLO[:, m], GHH[:, :], GHL[:, :], False, True).then_inc(o_done, 1)


def _const_table(np):
    t = np.zeros((P, CONSTS), np.float32)
    row, col = np.arange(P)[:, None], np.arange(256)[None, :]
    t[:, C_PAIR:C_PAIR + 256] = (row % PAIR // RANK == col // P) * LORA_SCALE
    t[:, C_DOWN:C_DOWN + TOK] = (row % (HS * RANK) // RANK == np.arange(TOK)[None, :] // P) * LORA_SCALE
    t[:, C_ID:C_ID + P] = np.eye(P)
    t[:, C_IOTA:C_IOTA + E] = np.arange(E)
    return t


def kernel(**inputs):
    import numpy as np
    import concourse.bacc as _bacc
    from concourse.bass_utils import run_bass_kernel_spmd as _run

    a = {k: np.asarray(v) for k, v in inputs.items()}

    def tiles(w):
        return w.T.reshape(-1, P, w.shape[0]).transpose(1, 0, 2)

    def padded(w, axis):
        pad = [(0, 0)] * w.ndim
        pad[axis] = (0, FC * P - F)
        return np.pad(w, pad)

    x = a["x"].reshape(HALVES, TOK, KD, P).transpose(0, 3, 2, 1)
    consts = _const_table(np)
    consts[:, C_BIAS:C_BIAS + KD] = a["L0_ffn_bias"].reshape(KD, P).T
    consts[:, C_BIAS + KD:C_BIAS + 2 * KD] = a["L1_ffn_b_base"].reshape(KD, P).T
    gu = [padded(a[f"L0_cond_W_{n}"], 0).reshape(FC, P, KD, P).transpose(0, 3, 2, 1) for n in ("gate", "up")]
    down = padded(a["L0_cond_W_down"], 1).T.reshape(FC, P, D)
    w_ffn = np.concatenate([np.stack(gu, 2).reshape(FC, P, GU), down], 2)
    a_gu = np.stack([a[f"L0_cond_A_{n}"][0].reshape(ADAPTERS, RANK, KD, P) for n in ("gate", "up")], 3)
    a_gu = a_gu.transpose(0, 4, 2, 3, 1).reshape(ADAPTERS, P, 2 * KD, RANK)
    b_gu = np.stack([padded(a[f"L0_cond_B_{n}"][0], 1).reshape(ADAPTERS, FC, P, RANK) for n in ("gate", "up")], 3)
    b_gu = b_gu.transpose(0, 1, 4, 3, 2).reshape(ADAPTERS, FC, RANK, 2 * P)
    a_dn = padded(a["L0_cond_A_down"][0], 2).reshape(ADAPTERS, RANK, FC, P).transpose(0, 3, 2, 1)
    a_sel = np.concatenate([a_gu.reshape(ADAPTERS, P, AG), a_dn.reshape(ADAPTERS, P, FC * RANK)], 2)
    b_dn = a["L0_cond_B_down"][0].transpose(0, 2, 1)
    q_w = np.ascontiguousarray(tiles(a["L0_ffn_quantized_weights"])).view(np.int32)
    blocks = D // 64
    q_scale = np.repeat(a["L0_ffn_scale_values"].reshape(D, blocks).T, 64, 0).reshape(KD, P, D).transpose(1, 0, 2)
    routers = np.stack([tiles(a["L1_cond_Wr"]), tiles(a["L1_ffn_W_router"])], 1)
    l1_w = np.stack([np.concatenate([tiles(a[w]).reshape(P, -1), tiles(a[la].reshape(E * RANK, D)).reshape(P, -1),
                                     a[lb].transpose(0, 2, 1).reshape(P, D)], 1)
                     for w, la, lb in (("L1_cond_W", "L1_cond_A", "L1_cond_B"), ("L1_ffn_W_base", "L1_ffn_A", "L1_ffn_B"))])
    ids = np.stack([a["itok_B_2_6"], a["itok_B_0_7"]])

    nc = _bacc.Bacc("TRN2", target_bir_lowering=False, num_devices=1)
    arrays, args = {}, []
    for name, v in (("x", x), ("ids", ids), ("consts", consts), ("a_sel", a_sel), ("b_gu", b_gu), ("b_dn", b_dn),
                    ("w_ffn", w_ffn), ("q_w", q_w), ("q_scale", q_scale), ("routers", routers), ("l1_w", l1_w)):
        v = np.ascontiguousarray(v)
        arrays[f"in_{name}"] = v
        args.append(nc.dram_tensor(f"in_{name}", v.shape, mybir.dt.from_np(v.dtype), kind="ExternalInput").ap())
    args.append(nc.dram_tensor("out_t", (HALVES, P, KD, TOK), F32, kind="ExternalOutput").ap())
    build(nc, *args)
    r = _run(nc, [arrays], core_ids=[0])
    o = np.asarray(r.results[0]["out_t"])
    return np.ascontiguousarray(o.transpose(0, 3, 2, 1)).reshape(B, P, D)
```

```python
from contextlib import ExitStack

import concourse.bass as bass
from concourse import mybir

F32 = mybir.dt.float32
F32R = mybir.dt.float32r
I32 = mybir.dt.int32
I8 = mybir.dt.int8
U32 = mybir.dt.uint32
ALU = mybir.AluOpType
ACT = mybir.ActivationFunctionType

P = 128
B = 8
D = 512
KD = D // P
HALVES = 2
HS = B // HALVES
TOK = HS * P
F = 1376
FC = -(-F // P)
RANK = 16
ADAPTERS = 16
E = 8
PAIR = 2 * RANK
GU = 2 * KD * P
AG = 2 * KD * RANK
LW = KD * D + KD * P + D
LORA_SCALE = 0.5
LANG_BIAS = 5.0
STEPS = HALVES * FC
LOOPED = 4
RC = PAIR + E
BLK = 32
NB = P // BLK
C_PAIR, C_DOWN, C_IOTA = 0, HS, 2 * HS
C_BIAS = C_IOTA + E
C_OWN = C_BIAS + 2 * KD
C_ID = C_OWN + HS * NB
C_SEL = C_ID + RC
CONSTS = C_SEL + P
WARMUP = 9


def build(nc, x, ids, consts, a_sel, b_gu, b_dn, w_ffn, q_w, q_scale, routers, l1_w, out):
    with ExitStack() as ctx:
        def sem(name):
            return ctx.enter_context(nc.semaphore(name))

        def sb(name, shape, dt=F32, where=ctx):
            return where.enter_context(nc.sbuf_tensor(name, shape, dt))

        ids_sb = sb("ids_sb", [1, 8], I32)
        lang_i = sb("lang_i", [P, B], I32)
        lang_f = sb("lang_f", [P, B])
        cst = sb("cst", [P, CONSTS])
        XF = sb("XF", [P, KD, HALVES * TOK])
        PH = sb("PH", [P, KD, HALVES * TOK], F32R)
        PL = sb("PL", [P, KD, HALVES * TOK], F32R)
        l1_raw = sb("l1_raw", [P, LW])
        q_i32 = sb("q_i32", [P, KD, D // 4], I32)
        q_sc = sb("q_sc", [P, KD, D])
        q_f = sb("q_f", [P, D])
        QH = sb("QH", [P, KD, D], F32R)
        QL = sb("QL", [P, KD, D], F32R)
        rt_raw = sb("rt_raw", [P, 2, KD, E])
        RT = sb("RT", [P, 2, KD, RC], F32R)
        SEL = sb("SEL", [P, P], F32R)
        warm = sb("warm", [P, 1])
        lang_bias = sb("lang_bias", [P, B, E])
        pair_mask = cst[:, C_PAIR:C_PAIR + HS]
        down_mask = cst[:, C_DOWN:C_DOWN + HS]
        own_block = cst[:, C_OWN:C_OWN + HS * NB]
        ident = cst[0:RC, C_ID:C_ID + RC]
        iota_e = cst[:, C_IOTA:C_IOTA + E]

        early = ctx.enter_context(ExitStack())
        w_raw = [sb(f"w_raw{i}", [P, GU + D], where=early) for i in range(2)]
        GUH = [sb(f"GUH{i}", [P, 2, KD, P], F32R, early) for i in range(2)]
        GUL = [sb(f"GUL{i}", [P, 2, KD, P], F32R, early) for i in range(2)]
        WDH = [sb(f"WDH{i}", [P, D], F32R, early) for i in range(2)]
        WDL = [sb(f"WDL{i}", [P, D], F32R, early) for i in range(2)]
        b_raw = [sb(f"b_raw{i}", [PAIR, 2, 2 * P], where=early) for i in range(2)]
        BGU = [sb(f"BGU{i}", [3 * PAIR, 2, 2 * P], F32R, early) for i in range(2)]
        sel_raw = sb("sel_raw", [P, B, AG + FC * RANK], where=early)
        a_raw = sel_raw[:, :, 0:AG].rearrange("p b (k r) -> p b k r", r=RANK)
        ad_raw = sel_raw[:, :, AG:].rearrange("p b (c r) -> p b c r", r=RANK)
        ADN = [sb(f"ADN{i}", [P, 2, HS * RANK], F32R, early) for i in range(2)]
        bd_raw = sb("bd_raw", [HS * RANK, HALVES, D], where=early)
        BD1 = sb("BD1", [P, HALVES, D], F32R, early)
        BD2 = sb("BD2", [P, HALVES, D], F32R, early)
        AH = sb("AH", [P, HALVES, 2 * KD, HS, RANK], F32R, early)
        AL = sb("AL", [P, HALVES, 2 * KD, HS, RANK], F32R, early)
        TM = sb("TM", [P, TOK], where=early)
        TH = sb("TH", [P, TOK], F32R, early)
        TL = sb("TL", [P, TOK], F32R, early)
        RGU = sb("RGU", [3 * PAIR, HALVES, 2, 2, 2 * P], F32R, early)
        TDM = sb("TDM", [P, TOK], where=early)
        TD1 = sb("TD1", [P, TOK], F32R, early)
        TD2 = sb("TD2", [P, TOK], F32R, early)
        sil = [sb(f"sil{i}", [P, TOK], where=early) for i in range(2)]
        act_f = [sb(f"act_f{i}", [P, TOK], where=early) for i in range(2)]
        ACH = [sb(f"ACH{i}", [P, TOK], F32R, early) for i in range(2)]
        ACL = [sb(f"ACL{i}", [P, TOK], F32R, early) for i in range(2)]
        early.close()

        UH = sb("UH", [P, KD, HALVES * TOK], F32R)
        UL = sb("UL", [P, KD, HALVES * TOK], F32R)
        LH = [sb(f"LH{i}", [P, LW], F32R) for i in range(2)]
        LL = [sb(f"LL{i}", [P, LW], F32R) for i in range(2)]
        hid = sb("hid", [P, TOK])
        gh = sb("gh", [P, TOK])
        GHH = sb("GHH", [P, TOK], F32R)
        GHL = sb("GHL", [P, TOK], F32R)
        route_t = sb("route_t", [RC, TOK])
        part_l = sb("part_l", [P, HS, E])
        logit = sb("logit", [P, HS, E])
        top8 = sb("top8", [P, HS, E])
        top8_i = sb("top8_i", [P, HS, E], U32)
        top2_f = sb("top2_f", [P, HS, 2])
        gap = sb("gap", [P, HS, 1])
        gap_e = sb("gap_e", [P, HS, 1])
        half_sum = sb("half_sum", [P, HS, 1])
        gate2 = sb("gate2", [P, HS, 2])
        onehot = sb("onehot", [P, HS, 2, E])
        chosen = sb("chosen", [P, HS, 2, E])
        gates = sb("gates", [P, HS, E])
        gates_t = sb("gates_t", [P, BLK])
        GTH = sb("GTH", [P, BLK], F32R)
        GTL = sb("GTL", [P, BLK], F32R)
        GSH = sb("GSH", [P, HS * NB, BLK], F32R)
        GSL = sb("GSL", [P, HS * NB, BLK], F32R)

        PB = [ctx.enter_context(nc.psum_tensor(f"bank{i}", [P, TOK], F32)) for i in range(8)]
        GATE, UP, TDN, TGU = PB[4], PB[5], PB[6], PB[7]
        ROUTE, HID, GATET, LOGITS = PB[4:8]

        ids_in, x_in, cst_in, lang_in = sem("ids_in"), [sem(f"x_in{k}") for k in range(HALVES * KD)], sem("cst_in"), sem("lang_in")
        a_in, bd_in, q_in, rt_in, gu0_in = [sem("a_in0"), sem("a_in1")], sem("bd_in"), sem("q_in"), sem("rt_in"), [sem("gate0_in"), sem("up0_in")]
        gu_in, dn_in, b_in = ([sem(f"{n}_in{i}") for i in range(2)] for n in ("gu", "dn", "b"))
        gu1_in, first_dn_in = sem("gu1_in"), [sem("first_dn_in0"), sem("first_dn_in1")]
        l1_in = [sem("l1_in0"), sem("l1_in1")]
        x_hi, x_split = sem("x_hi"), sem("x_split")
        a_hi, a_split = sem("a_hi"), sem("a_split")
        gate0_hi, gate0_split, warm_zero = sem("gate0_hi"), sem("gate0_split"), sem("warm_zero")
        gu_hi, gu_split, b_hi, b_split = sem("gu_hi"), sem("gu_split"), sem("b_hi"), sem("b_split")
        dn_hi, dn_split = sem("dn_hi"), sem("dn_split")
        bd_hi, bd_split = sem("bd_hi"), sem("bd_split")
        t_done, t_masked, t_hi, t_rest, r_hi, r_rest = (sem(n) for n in ("t_done", "t_masked", "t_hi", "t_rest", "r_hi", "r_rest"))
        gu_done, silu_done, act_done, act_hi, act_split = (sem(n) for n in ("gu_done", "silu_done", "act_done", "act_hi", "act_split"))
        dn_done, td_done, td_masked, td_hi, td_split, td_shift = (sem(n) for n in ("dn_done", "td_done", "td_masked", "td_hi", "td_split", "td_shift"))
        d_done, d_hi, d_split = sem("d_done"), sem("d_hi"), sem("d_split")
        q_prod, q_hi, q_split, rt_zero, rt_hi, rt_split = (sem(n) for n in ("q_prod", "q_hi", "q_split", "rt_zero", "rt_hi", "rt_split"))
        f_done, x2_done, u_hi, u_split = (sem(n) for n in ("f_done", "x2_done", "u_hi", "u_split"))
        l1_hi, l1_split = sem("l1_hi"), sem("l1_split")
        route_done, route_copied, logits_done, gap_done, exp_done, gates_done = (sem(n) for n in ("route_done", "route_copied", "logits_done", "gap_done", "exp_done", "gates_done"))
        hid_done, hid_copied, gatet_done, gh_done, gh_hi, gh_split = (sem(n) for n in ("hid_done", "hid_copied", "gatet_done", "gh_done", "gh_hi", "gh_split"))
        o_done, y_hi, y_split, x3_done, stored = (sem(n) for n in ("o_done", "y_hi", "y_split", "x3_done", "stored"))
        sel_ready, idle_zero = sem("sel_ready"), sem("idle_zero")
        chain = sem("chain")

        def half(h):
            return slice(h * TOK, (h + 1) * TOK)

        def f32(ap):
            return ap.bitcast(F32)

        def gate_bank(s):
            return PB[0] if isinstance(s, int) and s == 1 else GATE

        def up_bank(s):
            return PB[1] if isinstance(s, int) and s == 1 else UP

        def dyn(i):
            return bass.DynSlice(i, 1)

        def steps(eng, h, step, first=2, turns=LOOPED):
            with eng.Fori(0, turns) as i:
                for j in range(2):
                    k = h * FC + first + j
                    step(i * 2 + (first + j), i * 2 + k, k % 2, i + k // 2)

        def one_step(h, c, step):
            s = h * FC + c
            step(c, s, s % 2, s // 2)

        block = ctx.enter_context(nc.Block())

        @block.sync
        def _(sp):
            sp.dma_start(ids_sb[:, :], ids[0:1, :]).then_inc(ids_in, 16)
            for k in range(KD):
                if k < 2:
                    sp.dma_start(w_raw[0][:, k * GU // 2:(k + 1) * GU // 2], w_ffn[0, :, k * GU // 2:(k + 1) * GU // 2]).then_inc(gu0_in[k], 16)
                sp.dma_start(XF[:, k, half(0)], x[0, :, k, :]).then_inc(x_in[k], 16)
            sp.dma_start(w_raw[1][:, 0:GU], w_ffn[1, :, 0:GU]).then_inc(gu1_in, 16)
            sp.wait_ge(ids_in, 16)
            who = {}

            def load_b(c, par, h):
                for i in range(HS):
                    sp.dma_start(b_raw[par][RANK * (i % 2):RANK * (i % 2) + RANK, i // 2, :],
                                 b_gu[dyn(who[h * HS + i]), c].rearrange("a c r n -> r (a c n)")).then_inc(b_in[par], 16)

            for h in range(HALVES):
                for b in range(h * HS, (h + 1) * HS):
                    who[b] = sp.value_load(ids_sb[0:1, b:b + 1], min_val=0, max_val=ADAPTERS - 1)
                    sp.dma_start(sel_raw[:, b:b + 1, :], a_sel[dyn(who[b])].rearrange("a p n -> p a n")).then_inc(a_in[h], 16)
                load_b(slice(h, h + 1), h, 0)
            def load(h):
                def step(c, s, par, turn):
                    rows = w_ffn[dyn(c)].rearrange("a p n -> p (a n)")
                    sp.wait_ge(gu_split, s - 1)
                    sp.dma_start(w_raw[par][:, 0:GU], rows[:, 0:GU]).then_inc(gu_in[par], 16)
                    sp.wait_ge(b_split, s - 1)
                    load_b(dyn(c), par, h)
                    sp.wait_ge(dn_split, s - 1)
                    sp.dma_start(w_raw[par][:, GU:GU + D], rows[:, GU:GU + D]).then_inc(dn_in[par], 16)
                return step

            one_step(0, 2, load(0))
            one_step(0, 3, load(0))
            for b in range(B):
                sp.dma_start(bd_raw[RANK * (b % HS):RANK * (b % HS) + RANK, b // HS, :],
                             b_dn[dyn(who[b])].rearrange("a r n -> r (a n)")).then_inc(bd_in, 16)
            steps(sp, 0, load(0), first=4, turns=LOOPED - 1)
            one_step(0, FC - 1, load(0))
            sp.dma_start(q_i32[:, :, :], q_w[:, :, :]).then_inc(q_in, 16)
            sp.dma_start(q_sc[:, :, :], q_scale[:, :, :]).then_inc(q_in, 16)
            sp.dma_start(rt_raw[:, :, :, :], routers[:, :, :, :]).then_inc(rt_in, 16)
            sp.dma_start(l1_raw[:, :], l1_w[0]).then_inc(l1_in[0], 16)
            steps(sp, 1, load(1), first=0, turns=LOOPED + 1)
            one_step(1, FC - 1, load(1))
            sp.wait_ge(l1_split, 4)
            sp.dma_start(l1_raw[:, :], l1_w[1]).then_inc(l1_in[1], 16)
            for h in range(HALVES):
                for o in range(KD):
                    sp.wait_ge(x3_done, h * KD + o + 1)
                    sp.dma_start(out[h, :, o, :], XF[:, o, half(h)]).then_inc(stored, 16)
            sp.wait_ge(stored, 16 * HALVES * KD)

        @block.gpsimd
        def _(pool):
            nc.gpsimd.memset(f32(TD1[:, :]), 0.0).then_inc(idle_zero, 1)
            nc.gpsimd.memset(warm[:, :], 0.0).then_inc(warm_zero, 1)
            nc.gpsimd.memset(f32(RT[:, :, :, :]), 0.0).then_inc(rt_zero, 1)
            pool.wait_ge(x_in[1], 16)
            pool.dma_start(cst[:, :], consts[:, :]).then_inc(cst_in, 16)
            for k in range(KD):
                pool.dma_start(XF[:, k, half(1)], x[1, :, k, :]).then_inc(x_in[KD + k], 16)
            for s in range(2):
                pool.dma_start(w_raw[s][:, GU:GU + D], w_ffn[s, :, GU:GU + D]).then_inc(first_dn_in[s], 16)
            pool.dma_start(lang_i[:, :], ids[1:2, :].partition_broadcast(P)).then_inc(lang_in, 16)

        @block.scalar
        def _(act):
            def high(dst, src):
                return nc.scalar.activation(dst, src, ACT.Copy)

            act.wait_ge(warm_zero, 1)
            nc.scalar.activation(warm[:, :], warm[:, :], ACT.Silu)

            def split_x(h, ks=range(KD)):
                for k in ks:
                    act.wait_ge(x_in[h * KD + k], 16)
                    high(PH[:, k, half(h)], XF[:, k, half(h)]).then_inc(x_hi, 1)

            def split_a(h):
                act.wait_ge(a_in[h], 16 * HS)
                high(AH[:, h].rearrange("p k b r -> p b k r"), a_raw[:, h * HS:(h + 1) * HS]).then_inc(a_hi, 1)

            def split_gu(par):
                high(GUH[par][:, :, :, :].rearrange("p g k m -> p (g k m)"), w_raw[par][:, 0:GU]).then_inc(gu_hi, 1)

            def split_b(s, par, turn):
                act.wait_ge(b_in[par], (turn + 1) * 16 * HS)
                high(BGU[par][0:PAIR, :, :], b_raw[par][:, :, :])
                high(BGU[par][PAIR:2 * PAIR, :, :], b_raw[par][:, :, :]).then_inc(b_hi, 1)

            def rhs_gu(h):
                act.wait_ge(t_masked, h + 1)
                if h:
                    act.wait_ge(r_hi, h)
                high(TH[:, :], TM[:, :]).then_inc(t_hi, 1)
                act.wait_ge(t_rest, h + 1)
                for g in range(2):
                    for p in range(2):
                        q = PAIR * (2 * g + p)
                        last = high(RGU[PAIR:2 * PAIR, h, p, g, :], f32(TL[q:q + PAIR, 2 * P * p:2 * P * p + 2 * P]))
                last.then_inc(r_rest, 1)

            def split_down(h, c, s, par, turn):
                if not isinstance(s, int) or s >= 2:
                    act.wait_ge(dn_done, s - 1)
                if isinstance(s, int) and s < 2:
                    act.wait_ge(first_dn_in[par], 16)
                else:
                    act.wait_ge(dn_in[par], turn * 16)
                cs = slice(c, c + 1) if isinstance(c, int) else dyn(c)
                high(ADN[par][:, 0, :].rearrange("p (b r) -> p b r", r=RANK),
                     ad_raw[:, h * HS:(h + 1) * HS, cs, :].rearrange("p b c r -> p b (c r)"))
                high(WDH[par][:, :], w_raw[par][:, GU:GU + D]).then_inc(dn_hi, 1)

            def step_for(h):
                def step(c, s, par, turn, more=True, between=lambda: None):
                    if not isinstance(s, int) or s > 0:
                        split_down(h, c, s, par, turn)
                    if more:
                        nxt, nturn = 1 - par, turn + par
                        act.wait_ge(gu_in[nxt], nturn * 16)
                        if not isinstance(s, int) or s >= 1:
                            act.wait_ge(gu_done, s)
                        split_gu(nxt)
                        split_b(s + 1, nxt, nturn)
                    act.wait_ge(gu_done, s + 1)
                    nc.scalar.activation(sil[par][:, :], gate_bank(s)[:, :], ACT.Silu).then_inc(silu_done, 1)
                    between()
                    act.wait_ge(act_done, s + 1)
                    high(ACH[par][:, :], act_f[par][:, :]).then_inc(act_hi, 1)
                return step

            def down_rhs(h):
                act.wait_ge(td_masked, h + 1)
                high(TD1[:, :], TDM[:, :]).then_inc(td_hi, 1)
                high(TD2[64:128, :], TDM[0:64, :]).then_inc(td_shift, 1)

            def cond_out(h):
                for o in range(KD):
                    act.wait_ge(d_done, h * KD + o + 1)
                    high(PH[:, o, half(h)], PB[o][:, :]).then_inc(d_hi, 1)

            def split_q(ks):
                for k in ks:
                    act.wait_ge(q_prod, k + 1)
                    high(QH[:, k, :], q_f[:, :]).then_inc(q_hi, 1)

            act.wait_ge(gu0_in[0], 16)
            high(GUH[0][:, 0], w_raw[0][:, 0:GU // 2].rearrange("p (k m) -> p k m", k=KD)).then_inc(gate0_hi, 1)
            split_x(0, range(0, 1))
            act.wait_ge(gu0_in[1], 16)
            high(GUH[0][:, 1], w_raw[0][:, GU // 2:GU].rearrange("p (k m) -> p k m", k=KD)).then_inc(gu_hi, 1)
            split_x(0, range(1, KD))
            act.wait_ge(gu1_in, 16)
            split_gu(1)
            split_a(0)
            split_x(1, range(0, 2))
            split_b(0, 0, 0)
            split_x(1, range(2, KD))
            rhs_gu(0)
            split_a(1)
            one_step(0, 0, lambda *a: split_down(0, *a))
            one_step(0, 0, lambda *a: step_for(0)(*a, more=False, between=lambda: split_b(1, 1, 0)))
            one_step(0, 1, step_for(0))
            rhs_gu(1)
            steps(act, 0, step_for(0))
            act.wait_ge(bd_in, 16 * B)
            high(BD1[0:64, :, :], bd_raw[:, :, :])
            high(BD1[64:128, :, :], bd_raw[:, :, :])
            high(BD2[0:64, :, :], bd_raw[:, :, :]).then_inc(bd_hi, 1)
            one_step(0, FC - 1, step_for(0))
            down_rhs(0)
            one_step(1, 0, step_for(1))
            cond_out(0)
            one_step(1, 1, step_for(1))
            act.wait_ge(rt_in, 16)
            act.wait_ge(rt_zero, 1)
            for i in range(2):
                high(RT[:, i, :, 0:E], rt_raw[:, i, :, :]).then_inc(rt_hi, 1)
            split_q(range(0, 2))
            steps(act, 1, step_for(1))
            split_q(range(2, KD))
            one_step(1, FC - 1, lambda *a: step_for(1)(*a, more=False))
            down_rhs(1)

            def split_l1(i, q):
                n = LW // 4
                if q == 0:
                    act.wait_ge(l1_in[i], 16)
                high(LH[i][:, q * n:(q + 1) * n], l1_raw[:, q * n:(q + 1) * n]).then_inc(l1_hi, 1)

            def split_x2(t):
                h, o = divmod(t, KD)
                act.wait_ge(x2_done, t + 1)
                high(UH[:, o, half(h)], XF[:, o, half(h)]).then_inc(u_hi, 1)

            split_x2(0)
            split_x2(1)
            cond_out(1)
            for t in range(2, HALVES * KD):
                split_x2(t)
                if t < 6:
                    split_l1(0, t - 2)
            for i in range(2):
                for h in range(HALVES):
                    n = 2 * i + h
                    act.wait_ge(route_done, n + 1)
                    nc.scalar.activation(route_t[:, :], ROUTE[0:RC, :], ACT.Copy).then_inc(route_copied, 1)
                    act.wait_ge(gap_done, n + 1)
                    nc.scalar.activation(gap_e[:, :, :], gap[:, :, :], ACT.Exp).then_inc(exp_done, 1)
                    act.wait_ge(hid_done, n + 1)
                    if n:
                        act.wait_ge(gh_done, n)
                    nc.scalar.activation(hid[:, :], HID[:, :], ACT.Copy).then_inc(hid_copied, 1)
                    if n == 0:
                        split_l1(1, 0)
                        split_l1(1, 1)
                    act.wait_ge(gh_done, n + 1)
                    high(GHH[:, :], gh[:, :]).then_inc(gh_hi, 1)
                    if n == 0:
                        split_l1(1, 2)
                        split_l1(1, 3)
                    for o in range(KD):
                        if i == 0:
                            act.wait_ge(o_done, n * KD + o + 1)
                            high(PH[:, o, half(h)], PB[o][:, :]).then_inc(y_hi, 1)

        @block.vector
        def _(dve):
            count = [0]

            def link(ins):
                count[0] += 1
                ins.then_inc(chain, 1)
                dve.wait_ge(chain, count[0])

            def rest(dst, src, hi):
                return nc.vector.tensor_tensor(dst, src, f32(hi), ALU.subtract)

            def split_x(h, ks=range(KD)):
                for k in ks:
                    dve.wait_ge(x_hi, h * KD + k + 1)
                    rest(PL[:, k, half(h)], XF[:, k, half(h)], PH[:, k, half(h)]).then_inc(x_split, 1)

            def split_a(h):
                dve.wait_ge(a_hi, h + 1)
                rest(AL[:, h].rearrange("p k b r -> p b k r"), a_raw[:, h * HS:(h + 1) * HS],
                     AH[:, h].rearrange("p k b r -> p b k r")).then_inc(a_split, 1)

            def split_b(s, par):
                dve.wait_ge(b_hi, s + 1)
                rest(BGU[par][2 * PAIR:3 * PAIR, :, :], b_raw[par][:, :, :], BGU[par][0:PAIR, :, :]).then_inc(b_split, 1)

            def rhs_gu(h):
                dve.wait_ge(t_done, h + 1)
                if h:
                    dve.wait_ge(t_hi, h)
                nc.vector.tensor_tensor(TM[:, :].rearrange("p (b n) -> p b n", b=HS), TGU[:, :].rearrange("p (b n) -> p b n", b=HS),
                                        pair_mask.unsqueeze(2).to_broadcast([P, HS, P]), ALU.mult).then_inc(t_masked, 1)

                def rows(row, src, which):
                    for q in which:
                        g, p = divmod(q, 2)
                        last = nc.vector.tensor_copy(RGU[row:row + PAIR, h, p, g, :], src[q * PAIR:q * PAIR + PAIR, 2 * P * p:2 * P * p + 2 * P])
                    return last

                dve.wait_ge(t_masked, h + 1)
                rows(2 * PAIR, TM, range(0, 3))
                dve.wait_ge(t_hi, h + 1)
                if h:
                    dve.wait_ge(r_rest, h)
                rest(TL[:, :], TM[:, :], TH[:, :]).then_inc(t_rest, 1)
                rows(2 * PAIR, TM, range(3, 4))
                rows(0, TH, range(4)).then_inc(r_hi, 1)

            def split_gu(s, par):
                dve.wait_ge(gu_hi, s + 1)
                rest(GUL[par][:, :, :, :].rearrange("p g k m -> p (g k m)"), w_raw[par][:, 0:GU],
                     GUH[par][:, :, :, :].rearrange("p g k m -> p (g k m)")).then_inc(gu_split, 1)

            def split_down(h, c, s, par):
                dve.wait_ge(dn_hi, s + 1)
                cs = slice(c, c + 1) if isinstance(c, int) else dyn(c)
                rest(ADN[par][:, 1, :].rearrange("p (b r) -> p b r", r=RANK),
                     ad_raw[:, h * HS:(h + 1) * HS, cs, :].rearrange("p b c r -> p b (c r)"),
                     ADN[par][:, 0, :].rearrange("p (b r) -> p b r", r=RANK))
                rest(WDL[par][:, :], w_raw[par][:, GU:GU + D], WDH[par][:, :]).then_inc(dn_split, 1)

            def step_for(h):
                def step(c, s, par, turn, more=True, between=lambda: None):
                    if not isinstance(s, int) or s > 0:
                        split_down(h, c, s, par)
                    if more:
                        split_gu(s + 1, 1 - par)
                        split_b(s + 1, 1 - par)
                    dve.wait_ge(silu_done, s + 1)
                    nc.vector.tensor_tensor(act_f[par][:, :], sil[par][:, :], up_bank(s)[:, :], ALU.mult).then_inc(act_done, 1)
                    between()
                    dve.wait_ge(act_hi, s + 1)
                    rest(ACL[par][:, :], act_f[par][:, :], ACH[par][:, :]).then_inc(act_split, 1)
                return step
            def down_rhs(h):
                dve.wait_ge(td_done, h + 1)
                nc.vector.tensor_tensor(TDM[:, :].rearrange("p (b n) -> p b n", b=HS), TDN[:, :].rearrange("p (b n) -> p b n", b=HS),
                                        down_mask.unsqueeze(2).to_broadcast([P, HS, P]), ALU.mult).then_inc(td_masked, 1)
                dve.wait_ge(td_hi, h + 1)
                rest(TD2[0:64, :], TDM[0:64, :], TD1[0:64, :]).then_inc(td_split, 1)

            def cond_out(h):
                for o in range(KD):
                    dve.wait_ge(d_hi, h * KD + o + 1)
                    rest(PL[:, o, half(h)], PB[o][:, :], PH[:, o, half(h)]).then_inc(d_split, 1)

            def split_q(ks):
                for k in ks:
                    if k:
                        dve.wait_ge(q_split, k)
                    else:
                        dve.wait_ge(q_in, 32)
                    nc.vector.tensor_tensor(q_f[:, :], q_i32[:, k, :].bitcast(I8), q_sc[:, k, :], ALU.mult).then_inc(q_prod, 1)
                    dve.wait_ge(q_hi, k + 1)
                    rest(QL[:, k, :], q_f[:, :], QH[:, k, :]).then_inc(q_split, 1)

            def split_gu0(g):
                dve.wait_ge((gate0_hi, gu_hi)[g], 1)
                rest(GUL[0][:, g], w_raw[0][:, g * GU // 2:(g + 1) * GU // 2].rearrange("p (k m) -> p k m", k=KD), GUH[0][:, g]).then_inc((gate0_split, gu_split)[g], 1)

            split_gu0(0)
            split_x(0, range(0, 1))
            split_gu0(1)
            split_x(0, range(1, KD))
            split_gu(1, 1)
            split_a(0)
            split_x(1, range(0, 2))
            split_b(0, 0)
            split_x(1, range(2, KD))
            dve.wait_ge(cst_in, 16)
            rhs_gu(0)
            split_a(1)
            split_down(0, 0, 0, 0)
            one_step(0, 0, lambda *a: step_for(0)(*a, more=False, between=lambda: split_b(1, 1)))
            one_step(0, 1, step_for(0))
            rhs_gu(1)
            steps(dve, 0, step_for(0))
            dve.wait_ge(bd_hi, 1)
            rest(BD2[64:128, :, :], bd_raw[:, :, :], BD1[0:64, :, :]).then_inc(bd_split, 1)
            one_step(0, FC - 1, step_for(0))
            down_rhs(0)
            one_step(1, 0, step_for(1))
            cond_out(0)
            one_step(1, 1, step_for(1))
            for i in range(2):
                dve.wait_ge(rt_hi, i + 1)
                rest(RT[:, i, :, PAIR:RC], rt_raw[:, i, :, :], RT[:, i, :, 0:E]).then_inc(rt_split, 1)
            split_q(range(0, 2))
            nc.vector.tensor_copy(SEL[:, :], cst[:, C_SEL:C_SEL + P]).then_inc(sel_ready, 1)
            dve.wait_ge(lang_in, 16)
            link(nc.vector.tensor_copy(lang_f[:, :], lang_i[:, :]))
            link(nc.vector.tensor_tensor(lang_bias[:, :, :], iota_e.unsqueeze(1).to_broadcast([P, B, E]),
                                         lang_f[:, :].unsqueeze(2).to_broadcast([P, B, E]), ALU.is_equal))
            link(nc.vector.tensor_scalar(lang_bias[:, :, :], lang_bias[:, :, :], LANG_BIAS, None, ALU.mult))
            steps(dve, 1, step_for(1))
            split_q(range(2, KD))
            one_step(1, FC - 1, lambda *a: step_for(1)(*a, more=False))
            down_rhs(1)

            def split_l1(i, q):
                n = LW // 4
                dve.wait_ge(l1_hi, 4 * i + q + 1)
                rest(LL[i][:, q * n:(q + 1) * n], l1_raw[:, q * n:(q + 1) * n], LH[i][:, q * n:(q + 1) * n]).then_inc(l1_split, 1)

            def x2_tile(t):
                h, o = divmod(t, KD)
                dve.wait_ge(f_done, t + 1)
                nc.vector.scalar_tensor_tensor(XF[:, o, half(h)], PB[o if h else o + 4][:, :], cst[:, C_BIAS + o:C_BIAS + o + 1],
                                               XF[:, o, half(h)], ALU.add, ALU.add).then_inc(x2_done, 1)
                dve.wait_ge(u_hi, t + 1)
                rest(UL[:, o, half(h)], XF[:, o, half(h)], UH[:, o, half(h)]).then_inc(u_split, 1)

            x2_tile(0)
            x2_tile(1)
            cond_out(1)
            for t in range(2, HALVES * KD):
                x2_tile(t)
                if t < 6:
                    split_l1(0, t - 2)
            for i in range(2):
                for h in range(HALVES):
                    n = 2 * i + h
                    dve.wait_ge(logits_done, n + 1)
                    route = LOGITS[:, 0:HS * RC].rearrange("p (j c) -> p j c", c=RC)
                    if i == 0:
                        link(nc.vector.tensor_tensor(part_l[:, :, :], route[:, :, 0:E], lang_bias[:, h * HS:(h + 1) * HS, :], ALU.add))
                    else:
                        link(nc.vector.tensor_copy(part_l[:, :, :], route[:, :, 0:E]))
                    link(nc.vector.tensor_tensor(logit[:, :, :], part_l[:, :, :], route[:, :, PAIR:RC], ALU.add))
                    for j in range(HS):
                        last = nc.vector.max(top8[:, j, :], logit[:, j, :])
                    link(last)
                    nc.vector.tensor_tensor(gap[:, :, :], top8[:, :, 1:2], top8[:, :, 0:1], ALU.subtract).then_inc(gap_done, 1)
                    for j in range(HS):
                        last = nc.vector.max_index(top8_i[:, j, :], top8[:, j, :], logit[:, j, :])
                    link(last)
                    link(nc.vector.tensor_copy(top2_f[:, :, :], top8_i[:, :, 0:2]))
                    nc.vector.tensor_tensor(onehot[:, :, :, :], cst[:, C_IOTA:C_IOTA + E].unsqueeze(1).unsqueeze(1).to_broadcast([P, HS, 2, E]),
                                            top2_f[:, :, :].unsqueeze(3).to_broadcast([P, HS, 2, E]), ALU.is_equal)
                    dve.wait_ge(exp_done, n + 1)
                    link(nc.vector.tensor_scalar(half_sum[:, :, :], gap_e[:, :, :], 0.5, 0.5, ALU.mult, ALU.add))
                    link(nc.vector.reciprocal(gate2[:, :, 0:1], half_sum[:, :, :]))
                    link(nc.vector.tensor_tensor(gate2[:, :, 1:2], gate2[:, :, 0:1], gap_e[:, :, :], ALU.mult))
                    link(nc.vector.tensor_tensor(chosen[:, :, :, :], onehot[:, :, :, :], gate2[:, :, :].unsqueeze(3).to_broadcast([P, HS, 2, E]), ALU.mult))
                    link(nc.vector.tensor_tensor(gates[:, :, :], chosen[:, :, 0, :], chosen[:, :, 1, :], ALU.add))
                    link(nc.vector.transpose(gates_t[:, :], gates[:, :, :].rearrange("p j e -> p (j e)")))
                    link(nc.vector.tensor_copy(GTH[:, :], gates_t[:, :]))
                    link(rest(GTL[:, :], gates_t[:, :], GTH[:, :]))
                    for wide, narrow in ((GSH, GTH), (GSL, GTL)):
                        last = nc.vector.tensor_tensor(wide[:, :, :], f32(narrow[:, :]).unsqueeze(1).to_broadcast([P, HS * NB, BLK]),
                                                       own_block.unsqueeze(2).to_broadcast([P, HS * NB, BLK]), ALU.mult)
                    last.then_inc(gates_done, 1)
                    dve.wait_ge(gatet_done, n + 1)
                    dve.wait_ge(hid_copied, n + 1)
                    nc.vector.tensor_tensor(gh[:, :], hid[:, :], GATET[:, :], ALU.mult).then_inc(gh_done, 1)
                    dve.wait_ge(gh_hi, n + 1)
                    rest(GHL[:, :], gh[:, :], GHH[:, :]).then_inc(gh_split, 1)
                    if n == 0:
                        for q in range(4):
                            split_l1(1, q)
                    for o in range(KD):
                        if i == 0:
                            dve.wait_ge(y_hi, n * KD + o + 1)
                            rest(PL[:, o, half(h)], PB[o][:, :], PH[:, o, half(h)]).then_inc(y_split, 1)
                        else:
                            dve.wait_ge(o_done, n * KD + o + 1)
                            nc.vector.scalar_tensor_tensor(XF[:, o, half(h)], PB[o][:, :], cst[:, C_BIAS + KD + o:C_BIAS + KD + o + 1],
                                                           XF[:, o, half(h)], ALU.add, ALU.add).then_inc(x3_done, 1)

        @block.tensor
        def _(pe):
            def product(bank, wh, wl, mh, ml, start, stop):
                nc.tensor.matmul(bank, wh, mh, start=start, stop=False)
                nc.tensor.matmul(bank, wh, ml, start=False, stop=False)
                return nc.tensor.matmul(bank, wl, mh, start=False, stop=stop)

            def t_gu(h):
                pe.wait_ge(a_split, h + 1)
                pe.wait_ge(x_split, (h + 1) * KD)
                if h:
                    pe.wait_ge(t_masked, h)
                for k in range(KD):
                    cols = [t[:, h].rearrange("p k b r -> p k (b r)")[:, 2 * k:2 * k + 2, :] for t in (AH, AL)]
                    last = product(TGU[:, :], cols[0].rearrange("p g m -> p (g m)"), cols[1].rearrange("p g m -> p (g m)"),
                                   PH[:, k, half(h)], PL[:, k, half(h)], k == 0, k == KD - 1)
                last.then_inc(t_done, 1)

            def main_k(h, par, g, bank, k):
                product(bank[:, :], GUH[par][:, g, k, :], GUL[par][:, g, k, :], PH[:, k, half(h)], PL[:, k, half(h)], k == 0, k == KD - 1)

            def gate_up_main(h):
                def step(c, s, par, turn):
                    pe.wait_ge(gu_split, s + 1)
                    if isinstance(c, int) and c == 0:
                        pe.wait_ge(x_split, (h + 1) * KD)
                    for g, bank in enumerate((gate_bank(s), up_bank(s))):
                        if not isinstance(s, int) or s > 1:
                            pe.wait_ge((silu_done, act_done)[g], s)
                        for k in range(KD):
                            main_k(h, par, g, bank, k)
                return step

            def gate_up_lora(h):
                def step(c, s, par, turn):
                    pe.wait_ge(b_split, s + 1)
                    if isinstance(c, int) and c == 0:
                        pe.wait_ge(r_hi, h + 1)
                        pe.wait_ge(r_rest, h + 1)
                    for g, bank in enumerate((gate_bank(s), up_bank(s))):
                        for p in range(2):
                            last = nc.tensor.matmul(bank[:, 2 * P * p:2 * P * p + 2 * P], BGU[par][:, p, g * P:(g + 1) * P],
                                                    RGU[:, h, p, g, :], start=False, stop=True, skip_group_check=True)
                    last.then_inc(gu_done, 1)
                return step

            def down_a(h):
                def step(c, s, par, turn):
                    first = isinstance(c, int) and c == 0
                    final = isinstance(c, int) and c == FC - 1
                    pe.wait_ge(dn_split, s + 1)
                    pe.wait_ge(act_split, s + 1)
                    if first and h:
                        pe.wait_ge(td_masked, h)
                    nc.tensor.matmul(TDN[:, :], ADN[par][:, :, :].rearrange("p a m -> p (a m)"), ACH[par][:, :], start=first, stop=final, skip_group_check=True)
                    last = nc.tensor.matmul(TDN[0:64, :], ADN[par][:, 0, :], ACL[par][:, :], start=False, stop=final, skip_group_check=True)
                    if final:
                        last.then_inc(td_done, 1)
                return step

            def down_main(h):
                def step(c, s, par, turn):
                    first = isinstance(c, int) and c == 0
                    for o in (2, 3, 0, 1):
                        if first and h:
                            pe.wait_ge(d_split, KD)
                        elif first and o < 2:
                            pe.wait_ge((silu_done, act_done)[o], 2)
                        m = slice(o * P, (o + 1) * P)
                        last = product(PB[o][:, :], WDH[par][:, m], WDL[par][:, m], ACH[par][:, :], ACL[par][:, :], first, False)
                    last.then_inc(dn_done, 1)
                return step

            def down_lora(h):
                pe.wait_ge(bd_split, 1)
                pe.wait_ge(td_split, h + 1)
                pe.wait_ge(td_shift, h + 1)
                for o in range(KD):
                    m = slice(o * P, (o + 1) * P)
                    nc.tensor.matmul(PB[o][:, :], BD1[:, h, m], TD1[:, :], start=False, stop=False)
                    nc.tensor.matmul(PB[o][:, :], BD2[:, h, m], TD2[:, :], start=False, stop=True).then_inc(d_done, 1)

            def gate_up(h):
                def step(*a):
                    gate_up_main(h)(*a)
                    gate_up_lora(h)(*a)
                return step

            def down(h):
                def step(*a):
                    down_a(h)(*a)
                    down_main(h)(*a)
                return step

            def both(h):
                def step(c, s, par, turn):
                    gate_up(h)(c, s, par, turn)
                    down(h)(c - 1, s - 1, 1 - par, None)
                return step

            def ffn(t):
                h, o = divmod(t, KD)
                if o == 0:
                    pe.wait_ge(q_split, KD)
                    pe.wait_ge(d_split, (h + 1) * KD)
                m = slice(o * P, (o + 1) * P)
                for k in range(KD):
                    last = product(PB[o if h else o + 4][:, :], QH[:, k, m], QL[:, k, m], PH[:, k, half(h)], PL[:, k, half(h)], k == 0, k == KD - 1)
                last.then_inc(f_done, 1)

            pe.wait_ge(idle_zero, 1)
            for i in range(WARMUP):
                nc.tensor.matmul(TGU[:, :], TD1[:, 0:P], TD1[:, :], start=True, stop=True)
            for k in range(KD):
                for g, bank in enumerate((GATE, UP)):
                    pe.wait_ge((gate0_hi, gu_hi)[g], 1)
                    pe.wait_ge(x_hi, k + 1)
                    nc.tensor.matmul(bank[:, :], GUH[0][:, g, k, :], PH[:, k, half(0)], start=(k == 0), stop=False)
                    pe.wait_ge(x_split, k + 1)
                    nc.tensor.matmul(bank[:, :], GUH[0][:, g, k, :], PL[:, k, half(0)], start=False, stop=False)
                    pe.wait_ge((gate0_split, gu_split)[g], 1)
                    nc.tensor.matmul(bank[:, :], GUL[0][:, g, k, :], PH[:, k, half(0)], start=False, stop=(k == KD - 1))
            pe.wait_ge(gu_split, 2)
            for g, k in ((0, 0), (0, 1), (0, 2), (0, 3), (1, 0), (1, 1), (1, 2), (1, 3)):
                if (g, k) == (0, 2):
                    t_gu(0)
                main_k(0, 1, g, PB[g], k)
            one_step(0, 0, gate_up_lora(0))
            t_gu(1)
            one_step(0, 1, gate_up_lora(0))
            one_step(0, 0, down(0))
            steps(pe, 0, both(0))
            one_step(0, FC - 1, both(0))
            one_step(0, FC - 1, down_a(0))
            one_step(1, 0, gate_up(1))
            one_step(0, FC - 1, down_main(0))
            down_lora(0)
            one_step(1, 1, both(1))
            steps(pe, 1, both(1))
            one_step(1, FC - 1, both(1))
            one_step(1, FC - 1, down_a(1))
            one_step(1, FC - 1, down_main(1))
            ffn(0)
            ffn(1)
            down_lora(1)
            for t in range(2, HALVES * KD):
                if t == 2:
                    pe.wait_ge(td_masked, 2)
                ffn(t)

            pe.wait_ge(rt_split, 2)
            pe.wait_ge(sel_ready, 1)
            pe.wait_ge(cst_in, 16)
            for i in range(2):
                WH, WL = (t[:, 0:KD * D].rearrange("p (k n) -> p k n", k=KD) for t in (LH[i], LL[i]))
                AHI, ALO = (t[:, KD * D:KD * D + KD * P].rearrange("p (k n) -> p k n", k=KD) for t in (LH[i], LL[i]))
                BHI, BLO = (t[:, KD * D + KD * P:LW] for t in (LH[i], LL[i]))
                SH, SL = ((UH, UL), (PH, PL))[i]
                for h in range(HALVES):
                    n = 2 * i + h
                    pe.wait_ge((u_split, y_split)[i], (h + 1) * KD)
                    if n:
                        pe.wait_ge(gates_done, n)
                    for k in range(KD):
                        nc.tensor.matmul(ROUTE[0:RC, :], RT[:, i, k, :], SH[:, k, half(h)], start=(k == 0), stop=(k == KD - 1), skip_group_check=True)
                        last = nc.tensor.matmul(ROUTE[0:E, :], RT[:, i, k, 0:E], SL[:, k, half(h)], start=False, stop=(k == KD - 1), skip_group_check=True)
                    last.then_inc(route_done, 1)
                    pe.wait_ge(l1_split, 4 * i + 4)
                    if n:
                        pe.wait_ge(hid_copied, n)
                    for k in range(KD):
                        last = product(HID[:, :], AHI[:, k, :], ALO[:, k, :], SH[:, k, half(h)], SL[:, k, half(h)], k == 0, k == KD - 1)
                    last.then_inc(hid_done, 1)
                    pe.wait_ge(route_copied, n + 1)
                    for j in range(HS):
                        last = nc.tensor.transpose(LOGITS[:, j * RC:(j + 1) * RC], route_t[:, j * P:(j + 1) * P], ident)
                    last.then_inc(logits_done, 1)
                    for o in range(KD):
                        m = slice(o * P, (o + 1) * P)
                        if n == 0:
                            pe.wait_ge(x2_done, KD + o + 1)
                        elif n <= 2:
                            pe.wait_ge(y_split, (n - 1) * KD + o + 1)
                        else:
                            pe.wait_ge(x3_done, o + 1)
                        for k in range(KD):
                            product(PB[o][:, :], WH[:, k, m], WL[:, k, m], SH[:, k, half(h)], SL[:, k, half(h)], k == 0, False)
                        if o == 2:
                            pe.wait_ge(gates_done, n + 1)
                            if n:
                                pe.wait_ge(gh_done, n)
                            nc.tensor.matmul(GATET[:, :], SEL[:, :], GSH[:, :, :].rearrange("p g t -> p (g t)"), start=True, stop=False)
                            nc.tensor.matmul(GATET[:, :], SEL[:, :], GSL[:, :, :].rearrange("p g t -> p (g t)"), start=False, stop=True).then_inc(gatet_done, 1)
                    pe.wait_ge(gh_split, n + 1)
                    for o in range(KD):
                        m = slice(o * P, (o + 1) * P)
                        product(PB[o][:, :], BHI[:, m], BLO[:, m], GHH[:, :], GHL[:, :], False, True).then_inc(o_done, 1)


def _const_table(np):
    t = np.zeros((P, CONSTS), np.float32)
    row = np.arange(P)[:, None]
    sample = np.arange(HS)[None, :]
    t[:, C_PAIR:C_PAIR + HS] = (row % PAIR // RANK == sample % 2) * LORA_SCALE
    t[:, C_DOWN:C_DOWN + HS] = (row % (HS * RANK) // RANK == sample) * LORA_SCALE
    t[:, C_IOTA:C_IOTA + E] = np.arange(E)
    t[:, C_OWN:C_OWN + HS * NB] = row % BLK // E * NB + row // BLK == np.arange(HS * NB)[None, :]
    t[0:RC, C_ID:C_ID + RC] = np.eye(RC)
    t[:, C_SEL:C_SEL + P] = row % E == np.arange(P)[None, :] // RANK
    return t


def kernel(**inputs):
    import numpy as np
    import concourse.bacc as _bacc
    from concourse.bass_utils import run_bass_kernel_spmd as _run

    a = {k: np.asarray(v) for k, v in inputs.items()}

    def tiles(w):
        return w.T.reshape(-1, P, w.shape[0]).transpose(1, 0, 2)

    def padded(w, axis):
        pad = [(0, 0)] * w.ndim
        pad[axis] = (0, FC * P - F)
        return np.pad(w, pad)

    x = a["x"].reshape(HALVES, TOK, KD, P).transpose(0, 3, 2, 1)
    consts = _const_table(np)
    consts[:, C_BIAS:C_BIAS + KD] = a["L0_ffn_bias"].reshape(KD, P).T
    consts[:, C_BIAS + KD:C_BIAS + 2 * KD] = a["L1_ffn_b_base"].reshape(KD, P).T
    gu = [padded(a[f"L0_cond_W_{n}"], 0).reshape(FC, P, KD, P).transpose(0, 3, 2, 1) for n in ("gate", "up")]
    down = padded(a["L0_cond_W_down"], 1).T.reshape(FC, P, D)
    w_ffn = np.concatenate([np.stack(gu, 2).reshape(FC, P, GU), down], 2)
    a_gu = np.stack([a[f"L0_cond_A_{n}"][0].reshape(ADAPTERS, RANK, KD, P) for n in ("gate", "up")], 3)
    a_gu = a_gu.transpose(0, 4, 2, 3, 1).reshape(ADAPTERS, P, 2 * KD, RANK)
    b_gu = np.stack([padded(a[f"L0_cond_B_{n}"][0], 1).reshape(ADAPTERS, FC, P, RANK) for n in ("gate", "up")], 3)
    b_gu = b_gu.transpose(0, 1, 4, 3, 2).reshape(ADAPTERS, FC, RANK, 2 * P)
    a_dn = padded(a["L0_cond_A_down"][0], 2).reshape(ADAPTERS, RANK, FC, P).transpose(0, 3, 2, 1)
    a_sel = np.concatenate([a_gu.reshape(ADAPTERS, P, AG), a_dn.reshape(ADAPTERS, P, FC * RANK)], 2)
    b_dn = a["L0_cond_B_down"][0].transpose(0, 2, 1)
    q_w = np.ascontiguousarray(tiles(a["L0_ffn_quantized_weights"])).view(np.int32)
    blocks = D // 64
    q_scale = np.repeat(a["L0_ffn_scale_values"].reshape(D, blocks).T, 64, 0).reshape(KD, P, D).transpose(1, 0, 2)
    routers = np.stack([tiles(a["L1_cond_Wr"]), tiles(a["L1_ffn_W_router"])], 1)
    l1_w = np.stack([np.concatenate([tiles(a[w]).reshape(P, -1), tiles(a[la].reshape(E * RANK, D)).reshape(P, -1),
                                     a[lb].transpose(0, 2, 1).reshape(P, D)], 1)
                     for w, la, lb in (("L1_cond_W", "L1_cond_A", "L1_cond_B"), ("L1_ffn_W_base", "L1_ffn_A", "L1_ffn_B"))])
    ids = np.stack([a["itok_B_2_6"], a["itok_B_0_7"]])

    nc = _bacc.Bacc("TRN2", target_bir_lowering=False, num_devices=1)
    arrays, args = {}, []
    for name, v in (("x", x), ("ids", ids), ("consts", consts), ("a_sel", a_sel), ("b_gu", b_gu), ("b_dn", b_dn),
                    ("w_ffn", w_ffn), ("q_w", q_w), ("q_scale", q_scale), ("routers", routers), ("l1_w", l1_w)):
        v = np.ascontiguousarray(v)
        arrays[f"in_{name}"] = v
        args.append(nc.dram_tensor(f"in_{name}", v.shape, mybir.dt.from_np(v.dtype), kind="ExternalInput").ap())
    args.append(nc.dram_tensor("out_t", (HALVES, P, KD, TOK), F32, kind="ExternalOutput").ap())
    build(nc, *args)
    r = _run(nc, [arrays], core_ids=[0])
    o = np.asarray(r.results[0]["out_t"])
    return np.ascontiguousarray(o.transpose(0, 3, 2, 1)).reshape(B, P, D)
```
